# Optimizing a Trainium2 kernel written in Bass

```python
import numpy as np
import jax
import jax.numpy as jnp

def _softmax(x, axis=-1):
    return jax.nn.softmax(x, axis=axis)

def _gelu(x):
    return jax.nn.gelu(x, approximate=True)

def _silu(x):
    return jax.nn.silu(x)

def _sigmoid(x):
    return jax.nn.sigmoid(x)

def _layernorm(x, axis=-1, eps=1e-05):
    m = jnp.mean(x, axis=axis, keepdims=True)
    v = jnp.var(x, axis=axis, keepdims=True)
    return (x - m) / jnp.sqrt(v + eps)

def _scatter_add(tgt, idx, src, axis=0):
    return tgt.at[idx].add(src)

def _segment_sum(src, seg, n):
    return jax.ops.segment_sum(src, seg, n)
kernel_name = 'mk_cond_resid_d2_seqx_r4_e851e7'

def setup_inputs(seed: int=0):
    np.random.seed(seed)
    _w = jnp.asarray

    def _rec_inputs():
        import jax
        import jax.numpy as jnp
        _rk = jax.random.key(seed)
        x = -0.0002928 + 1 * jax.random.normal(jax.random.fold_in(_rk, 1), (32, 256, 256), jnp.float32)
        _lenS = 256 - jax.random.randint(jax.random.fold_in(_rk, 7), (32,), 0, max(1, 256 // 4) + 1, jnp.int32)
        _lenS2 = 256 - jax.random.randint(jax.random.fold_in(_rk, 8), (32,), 0, max(1, 256 // 4) + 1, jnp.int32)
        cond_1024 = 0.0061147 + 1.02565 * jax.random.normal(jax.random.fold_in(_rk, 11), (32, 256), jnp.float32)
        return (x, cond_1024)
    x, cond_1024 = _rec_inputs()

    def _L0_cond_setup():
        import jax, jax.numpy as jnp
        import numpy as np
        D, HS, HE, E, K = (256, 512, 256, 8, 2)
        B, T = (4, 256)
        N_SHARED = 1
        key = jax.random.key(seed)
        ks = jax.random.split(key, 9)
        g = lambda k, shape, s: jax.random.normal(k, shape, jnp.float32) * s
        return {'x': g(ks[0], (B, T, D), 1.0), 't_emb': g(ks[1], (B, D), 1.0), 'router_W': g(ks[2], (2 * D, E), 0.01), 'router_bias': jnp.zeros((E,), jnp.float32), 'w1': g(ks[3], (D, HS), 0.02), 'w3': g(ks[4], (D, HS), 0.02), 'w2': g(ks[5], (HS, D), 0.02), 'W1e': g(ks[6], (E, D, HE), 0.02), 'W2e': g(ks[7], (E, HE, D), 0.02)}
    _L0_cond_all = _L0_cond_setup()
    _L0_cond_in = {k: v for k, v in _L0_cond_all.items() if k in ('router_W', 'router_bias', 'w1', 'w3', 'w2', 'W1e', 'W2e')}
    del _L0_cond_all

    def _L1_cond_setup():
        import jax, jax.numpy as jnp
        import numpy as np
        LATENT = 256
        key = jax.random.key(seed)
        k1, k2, k3, k4 = jax.random.split(key, 4)
        B, T, D = (64, 128, LATENT)
        h_t = jax.random.normal(k1, (B, D), dtype=jnp.float32)
        z = jax.random.normal(k2, (B, T, D), dtype=jnp.float32)
        bound = 1.0 / np.sqrt(2 * D)
        W = jax.random.uniform(k3, (D, 2 * D), minval=-bound, maxval=bound, dtype=jnp.float32)
        b = jax.random.uniform(k4, (D,), minval=-bound, maxval=bound, dtype=jnp.float32)
        alpha = jnp.full((D,), 0.1, dtype=jnp.float32)
        return {'h_t': h_t, 'z': z, 'W': W, 'b': b, 'alpha': alpha}
    _L1_cond_all = _L1_cond_setup()
    _L1_cond_in = {k: v for k, v in _L1_cond_all.items() if k in ('W', 'b', 'alpha')}
    del _L1_cond_all
    return {'x': x, 'cond_1024': cond_1024, 'L0_cond_router_W': _L0_cond_in['router_W'], 'L0_cond_router_bias': _L0_cond_in['router_bias'], 'L0_cond_w1': _L0_cond_in['w1'], 'L0_cond_w3': _L0_cond_in['w3'], 'L0_cond_w2': _L0_cond_in['w2'], 'L0_cond_W1e': _L0_cond_in['W1e'], 'L0_cond_W2e': _L0_cond_in['W2e'], 'L1_cond_W': _L1_cond_in['W'], 'L1_cond_b': _L1_cond_in['b'], 'L1_cond_alpha': _L1_cond_in['alpha']}

def reference(x, cond_1024, L0_cond_router_W, L0_cond_router_bias, L0_cond_w1, L0_cond_w3, L0_cond_w2, L0_cond_W1e, L0_cond_W2e, L1_cond_W, L1_cond_b, L1_cond_alpha):
    import jax
    import jax.numpy as jnp

    def _L0_cond_ref(x, t_emb, router_W, router_bias, w1, w3, w2, W1e, W2e):
        import jax, jax.numpy as jnp
        import numpy as np
        D, HS, HE, E, K = (256, 512, 256, 8, 2)
        B, T = (4, 256)
        N_SHARED = 1
        Bb, Tt, C = x.shape
        xf = x.reshape(-1, C)
        tf = jnp.broadcast_to(t_emb[:, None, :], (Bb, Tt, C)).reshape(-1, C)
        N = xf.shape[0]
        shared = jax.nn.silu(xf @ w1) * (xf @ w3) @ w2
        s = jax.nn.sigmoid((jnp.concatenate([xf, tf], axis=-1) @ router_W).astype(jnp.float32))
        sel_scores = s + router_bias
        _, topk_idx = jax.lax.top_k(sel_scores, K)
        s_sel = jnp.take_along_axis(s, topk_idx, axis=1)
        denom = s_sel.sum(axis=1, keepdims=True)
        gates = jnp.where(denom > 1e-09, s_sel / (denom + 1e-09), 1.0 / K).astype(x.dtype)
        combine = jnp.zeros((N, E), x.dtype).at[jnp.arange(N)[:, None], topk_idx].add(gates)
        h = jax.nn.gelu(jnp.einsum('nc,ech->enh', xf, W1e), approximate=False)
        y = jnp.einsum('enh,ehc->enc', h, W2e)
        routed = jnp.einsum('ne,enc->nc', combine, y)
        return ((shared + routed) / (N_SHARED + K)).reshape(Bb, Tt, C)

    def _L1_cond_ref(h_t, z, W, b, alpha):
        import jax, jax.numpy as jnp
        import numpy as np
        LATENT = 256
        D = h_t.shape[-1]
        Wh = W[:, :D]
        Wz = W[:, D:]
        leak = 1.0 - alpha

        def step(h, z_t):
            gate = jax.nn.sigmoid(h @ Wh.T + z_t @ Wz.T + b)
            h_new = jnp.tanh(h * leak + gate * z_t)
            return (h_new, h_new)
        _, hs = jax.lax.scan(step, h_t, jnp.swapaxes(z, 0, 1))
        return jnp.swapaxes(hs, 0, 1)
    x = x + _L0_cond_ref(x, cond_1024, L0_cond_router_W, L0_cond_router_bias, L0_cond_w1, L0_cond_w3, L0_cond_w2, L0_cond_W1e, L0_cond_W2e)
    x = x + _L1_cond_ref(cond_1024, x, L1_cond_W, L1_cond_b, L1_cond_alpha)
    return x

_drawn_inputs = setup_inputs


def setup_inputs(seed=0):
    import zlib

    import numpy as np

    out = dict(_drawn_inputs(seed))
    spreads = {'L0_cond_router_bias': (0.0, 0.548), 'L1_cond_alpha': (0.10000000149011612, 0.6)}
    factors = {'L0_cond_router_W': 7.679,
     'L0_cond_w1': 7.038,
     'L0_cond_w3': 6.938,
     'L0_cond_w2': 6.949,
     'L0_cond_W1e': 4.391,
     'L0_cond_W2e': 4.18,
     'L1_cond_b': 47.419}
    for name, (base, spread) in spreads.items():
        noise = np.random.default_rng([zlib.crc32(name.encode()), seed]).standard_normal(out[name].shape)
        drawn = base * np.exp(spread * noise) if base else spread * noise
        out[name] = jnp.asarray(drawn.astype(out[name].dtype))
    for name, factor in factors.items():
        out[name] = (out[name] * factor).astype(out[name].dtype)
    return out
```

```python
from contextlib import ExitStack

import concourse.bass as bass
from concourse import mybir

F32 = mybir.dt.float32
F16 = mybir.dt.float16
ALU = mybir.AluOpType
ACT = mybir.ActivationFunctionType
AX_X = mybir.AxisListType.X

P = 128
TOPK = 2
N_SHARED = 1

EXPERT, SHARED = "expert", "shared"
UNITS = []
for _n in range(4):
    UNITS += [(EXPERT, 4 * _n + _m) for _m in range(4)] + [(SHARED, _n)]
NU = len(UNITS)
DOWN_LAG = 2
REC_SLOT = 4

TURN_X, OUT, LOGITS, TURN_G, SPREAD = "turn_x", "out", "logits", "turn_g", "spread"
SPARE = [(OUT, 1, 1), (TURN_X, 0, 3), (TURN_X, 1, 4), (LOGITS, 0, 6), (TURN_G, 0, 11),
         (SPREAD, 0, 12), (SPREAD, 1, 13), (OUT, 0, 14), (SPREAD, 2, 14), (SPREAD, 3, 15),
         (SPREAD, 4, 16), (SPREAD, 5, 17), (SPREAD, 6, 18), (SPREAD, 7, 19)]
SIGMOID_SLOT = 7
ROUTE_SLOT = 8

TAKEN = 3.0e38
PAD = -3.0e38
N_CONST = 27


def moe_gated_recurrence(nc, x, cond, router_w, router_b, w1, w3, w2, w1e, w2e, gate_w, gate_b, alpha, out):
    NB, T, C = x.shape
    E, _, HE = w1e.shape
    HS = w1.shape[1]
    SMALL = 7
    KC = C // P
    TT = P // NB
    NJ = 4
    TG = NJ * TT
    G = NJ * P
    NG = T // TG
    HALF = TG // 2
    STEP = KC * NB
    MID = HS // P
    assert KC == 2 and HE == 2 * P and MID == 4 and E == 8 and NG == 16
    assert sum(k == EXPERT for k, _ in UNITS) == E * HE // P

    WUP = 64.0
    UP = 0.5 * WUP
    WDN = 64.0
    MEAN = 0.5 / ((N_SHARED + TOPK) * WDN)

    x_in = x.rearrange("b (g j t) c -> g t b j c", j=NJ, t=TT)
    out_v = out.rearrange("b (g h j t) c -> g h t b j c", h=2, j=NJ // 2, t=TT)

    with ExitStack() as ctx:
        def sb(name, shape, dt=F32):
            return ctx.enter_context(nc.sbuf_tensor(name, shape, dt))

        def sem(name):
            return ctx.enter_context(nc.semaphore(name))

        bank = [ctx.enter_context(nc.psum_tensor(f"bank{i}", [P, 512], F32)) for i in range(8)]
        up_ps = bank[0:2]
        y_ps = bank[2:4]
        gate_ps = bank[4:6]
        spare = bank[6:8]

        NSTAGE = 4
        stage = sb("stage", [P, NSTAGE, 1024])
        w1e_s = [sb(f"w1e_{h}", [P, E, KC, HE], F16) for h in ("high", "low")]
        w2e_s = [sb(f"w2e_{h}", [P, E, KC, C], F16) for h in ("high", "low")]
        w13_s = [sb(f"w13_{h}", [P, 2, KC, HS], F16) for h in ("high", "low")]
        w2_s = [sb(f"w2_{h}", [P, MID, C], F16) for h in ("high", "low")]
        gw = sb("gw", [P, KC, 2 * C])
        gwt = [sb(f"gwt_{h}", [P, 2 * KC, C], F16) for h in ("high", "low")]
        rw = sb("rw", [P, 2 * KC, E])
        rwx = sb("rwx", [P, KC, E])
        gb_in = sb("gb_in", [2, C])
        gb_full = sb("gb_full", [2, C])
        gb_hi = sb("gb_hi", [2, C], F16)
        gb_lo = sb("gb_lo", [2, C], F16)
        gb_lo2 = sb("gb_lo2", [2, C], F16)
        gb = sb("gb", [2, C], F16)
        ones2 = sb("ones2", [2, HALF * NB], F16)
        al = sb("al", [P, KC])
        al1 = sb("al1", [P, KC])
        ones = sb("ones", [P, P])
        leak = sb("leak", [P, KC, NB])
        ident = sb("ident", [P, P])
        ident16 = sb("ident16", [P, P], F16)
        pick2 = sb("pick2", [16, E])
        pick = sb("pick", [16, E, P], F16)
        cond_in = sb("cond_in", [NB, C])
        cond_t = sb("cond_t", [P, KC, TT, NB])
        cond_lg = sb("cond_lg", [P, NJ, E])
        rbias = sb("rbias", [P, NJ, E])

        x_tok = sb("x_tok", [P, 2, NJ, C])
        xq = sb("xq", [P, 2, KC, G])
        xs = [sb(f"xs_{h}", [P, 2, KC, G], F16) for h in ("high", "low")]
        lg = sb("lg", [P, NJ, E])
        sg = sb("sg", [P, NJ, E])
        sel = sb("sel", [P, NJ, 16])
        top8 = sb("top8", [P, NJ, 8])
        seek = sb("seek", [P, NJ, 8])
        left = sb("left", [P, NJ, 16])
        fence = sb("fence", [P, 1])
        mask = sb("mask", [P, NJ, E])
        smask = sb("smask", [P, NJ, E])
        den = sb("den", [P, NJ])
        deps = sb("deps", [P, NJ])
        drec = sb("drec", [P, NJ])
        okay = sb("okay", [P, NJ])
        okrec = sb("okrec", [P, NJ])
        alt = sb("alt", [P, NJ])
        part_a = sb("part_a", [P, NJ, E])
        part_b = sb("part_b", [P, NJ, E])
        comb = sb("comb", [P, NJ, E])
        comb16 = sb("comb16", [P, NJ, 2, E], F16)
        combt = sb("combt", [16, G], F16)
        spread = sb("spread", [P, 2, E, G])
        NH, NR = 2, 4
        act32 = sb("act32", [P, NH, G])
        half32 = sb("half32", [P, G])
        prod32 = sb("prod32", [P, NH, G])
        hid = [sb(f"hid_{h}", [P, NR, G], F16) for h in ("high", "low")]
        zq = sb("zq", [P, 2, TG, KC, NB])
        zs = [sb(f"zs_{h}", [P, TG, KC, NB], F16) for h in ("high", "low")]
        hist = sb("hist", [P, TG, KC, NB])
        hs = [sb(f"hs_{h}", [P, 2, KC, NB], F16) for h in ("high", "low")]
        th = sb("th", [P, 2, KC, NB])
        gz = sb("gz", [P, KC, NB])
        pre = sb("pre", [P, 2, KC, NB])
        hl = sb("hl", [P, 2, KC, NB])
        o_ch = sb("o_ch", [P, KC, HALF, NB])
        o_tok = sb("o_tok", [P, 2, 2, C])

        s_x = [sem("s_x_even"), sem("s_x_odd")]
        s_rw = sem("s_rw")
        s_small = sem("s_small")
        s_cond = sem("s_cond")
        s_gw = sem("s_gw")
        s_stage = [sem(f"s_stage{i}") for i in range(NSTAGE)]
        s_ident = sem("s_ident")
        s_const = sem("s_const")
        s_convhi = sem("s_convhi")
        s_conv = sem("s_conv")
        s_turn0 = sem("s_turn0")
        s_gwhi = sem("s_gwhi")
        s_gwlo = sem("s_gwlo")
        s_condt = sem("s_condt")
        s_clg_ps = sem("s_clg_ps")
        s_up = sem("s_up")
        s_gelu = sem("s_gelu")
        s_tanh = sem("s_tanh")
        s_su = sem("s_su")
        s_prod = sem("s_prod")
        s_hi = sem("s_hi")
        s_lo = sem("s_lo")
        s_down = sem("s_down")
        s_z = sem("s_z")
        s_zhi = sem("s_zhi")
        s_zlo = sem("s_zlo")
        s_step = sem("s_step")
        s_th = sem("s_th")
        s_gz = sem("s_gz")
        s_pre = sem("s_pre")
        s_h = sem("s_h")
        s_hhi = sem("s_hhi")
        s_hlo = sem("s_hlo")
        s_hl = sem("s_hl")
        s_turnx = sem("s_turnx")
        s_xq = sem("s_xq")
        s_xhi = sem("s_xhi")
        s_xlo = sem("s_xlo")
        s_lgps = sem("s_lgps")
        s_lg = sem("s_lg")
        s_sg = sem("s_sg")
        s_route = sem("s_route")
        s_gates = sem("s_gates")
        s_comb = sem("s_comb")
        s_turng = sem("s_turng")
        s_combt = sem("s_combt")
        s_sprps = sem("s_sprps")
        s_spr = sem("s_spr")
        s_och = sem("s_och")
        s_turno = sem("s_turno")
        s_otok = sem("s_otok")
        s_out = [sem("s_out_first"), sem("s_out_second")]

        class Body:
            def __init__(self, g, n, loads=None):
                self.g, self.n = g, n
                self.loads = (n + 1) // 2 + 1 if loads is None else loads
                self.units = n < NG
                self.tail = 1 <= n <= NG
                self.prep = n + 1 < NG
                self.late = 2 <= n <= NG + 1

            def there(self, what, part, n):
                if what == OUT:
                    return (1 <= n <= NG) if part == 0 else (2 <= n <= NG + 1)
                return 0 <= n + 1 < NG

        def released(eng, body, pos):
            p, back = pos - 2, 0
            while True:
                if p < 0:
                    p += len(SPARE)
                    back += 1
                n = body.n - back
                if n < -1:
                    return
                what, part, _ = SPARE[p]
                if body.there(what, part, n):
                    break
                p -= 2
            g = (body.g - back - 1 - part) if what == OUT else (body.g - back + 1)
            if what == TURN_X:
                eng.wait_ge(s_xhi, g * KC + part + 1)
            elif what == OUT:
                eng.wait_ge(s_otok, g * 2 + part + 1)
            elif what == LOGITS:
                eng.wait_ge(s_lg, g + 1)
            elif what == TURN_G:
                eng.wait_ge(s_combt, g + 1)
            else:
                eng.wait_ge(s_spr, g * E + part + 1)

        ring_at, at = [], 0
        for kind, _ in UNITS:
            ring_at.append(at)
            at += 1 if kind == EXPERT else 2
        assert at % 2 == 0
        n_exp = [sum(k == EXPERT for k, _ in UNITS[:u + 1]) for u in range(NU)]
        n_sha = [sum(k == SHARED for k, _ in UNITS[:u + 1]) for u in range(NU)]
        NE, NS = n_exp[-1], n_sha[-1]

        CONV = [("w1e", 0), ("w2e", 0), ("w1e", 1), ("w2e", 1), ("w13", 0), ("w13", 1), ("w2", 0)]
        for e in range(2, E):
            CONV += [("w1e", e), ("w2e", e)]
        CONV_AT = {key: n for n, key in enumerate(CONV)}

        def conv_parts(key):
            kind, i = key
            if kind == "w1e":
                src, dst = w1e[i].rearrange("(k p) h -> p k h", p=P), [w[:, i] for w in w1e_s]
            elif kind == "w2e":
                src, dst = w2e[i].rearrange("(k p) h -> p k h", p=P), [w[:, i] for w in w2e_s]
            elif kind == "w13":
                src, dst = (w1, w3)[i].rearrange("(k p) h -> p k h", p=P), [w[:, i] for w in w13_s]
            else:
                src, dst = w2.rearrange("(k p) h -> p k h", p=P), [w[:, :, :] for w in w2_s]
            k, w = src.shape[1], src.shape[2]
            return src, [d.rearrange("p k h -> p (k h)") for d in dst], k, w

        def conv_ready(eng, n, key):
            if n == 0:
                eng.wait_ge(s_conv, CONV_AT[key] + 1)

        def run_bodies(eng, body):
            for n in range(3):
                body(Body(n, n))
            with eng.Fori(1, NG // 2 - 1) as i:
                body(Body(i * 2 + 1, 3, i + 2))
                body(Body(i * 2 + 2, 4, i + 2))
            for n in range(NG - 1, NG + 2):
                body(Body(n, n))

        def bcast(ap):
            return ap[:].rearrange("p (j a) -> p j a", a=1).broadcast_to([P, NJ, E])

        def flat(ap):
            return ap.rearrange("p t k b -> p (t k b)")

        def flat3(ap):
            return ap.rearrange("p k b -> p (k b)")

        def gate_sums(s):
            at_col = (s % HALF) * STEP
            return gate_ps[s // HALF][:, at_col:at_col + STEP]

        def gate_view(pos):
            return spare[pos % 2][0:16, 0:G // 2].bitcast(F16)

        def spare_at(what, part=0):
            return [p for p, u in enumerate(SPARE) if u[:2] == (what, part)][0]

        block = ctx.enter_context(nc.Block())

        @block.sync
        def _(sp):
            def load_x(g, par):
                for t in range(TT):
                    sp.dma_start(x_tok[NB * t:NB * (t + 1), par, :, :], x_in[g, t]).then_inc(s_x[par], 16)

            def load_weight(n):
                src, _, k, w = conv_parts(CONV[n])
                if n >= NSTAGE:
                    sp.wait_ge(s_conv, n - NSTAGE + 1)
                sp.dma_start(stage[:, n % NSTAGE, 0:k * w].rearrange("p (k w) -> p k w", k=k),
                             src).then_inc(s_stage[n % NSTAGE], 16)

            def body(b):
                if b.prep:
                    if b.n >= 1:
                        sp.wait_ge(s_turnx, b.g * KC)
                    load_x(b.g + 1, (b.n + 1) % 2)
                for part, there, g in ((1, b.late, b.g - 2), (0, b.tail, b.g - 1)):
                    if there:
                        sp.wait_ge(s_otok, g * 2 + part + 1)
                        for t in range(TT):
                            sp.dma_start(out_v[g, part, t], o_tok[NB * t:NB * (t + 1), part, :, :]
                                         ).then_inc(s_out[part], 16)

            sp.dma_start(cond_in[:], cond).then_inc(s_cond, 16)
            load_x(0, 0)
            sp.dma_start(rw[:], router_w.rearrange("(k p) e -> p k e", p=P)).then_inc(s_rw, 16)
            for n in range(NSTAGE):
                load_weight(n)
            for n in range(NSTAGE, 7):
                load_weight(n)
            sp.dma_start(gw[:], gate_w.rearrange("(k p) c -> p k c", p=P)).then_inc(s_gw, 16)
            for n in range(7, len(CONV)):
                load_weight(n)
            run_bodies(sp, body)
            for part in range(2):
                sp.wait_ge(s_out[part], 16 * TT * NG)

        @block.gpsimd
        def _(pool):
            for i in range(NJ):
                pool.dma_start(rbias[:, i, :], router_b.rearrange("(a e) -> a e", a=1).broadcast_to([P, E])
                               ).then_inc(s_small, 16)
            for k in range(KC):
                pool.dma_start(al[:, k:k + 1], alpha.rearrange("(k p a) -> k p a", p=P, a=1)[k]).then_inc(s_small, 16)
            pool.dma_start(gb_in[:], gate_b.rearrange("(a c) -> a c", a=1).broadcast_to([2, C])
                           ).then_inc(s_small, 16)
            nc.gpsimd.memset(ident[:], 0.0).then_inc(s_ident, 1)
            pool.wait_ge(s_ident, 1)
            nc.gpsimd.affine_select(out=ident[:], in_=ident[:], compare_op=ALU.not_equal, fill=1.0,
                                    base=0, pattern=[[-1, P]], channel_multiplier=1).then_inc(s_ident, 1)

            def body(b):
                if not b.tail:
                    return
                for s in range(TG):
                    pool.wait_ge(s_h, (b.g - 1) * TG + s + 1)
                    nc.gpsimd.tensor_tensor(hl[:, s % 2], hist[:, (s - 1) % TG], leak[:], ALU.mult
                                            ).then_inc(s_hl, 1)

            pool.wait_ge(s_const, N_CONST)
            run_bodies(pool, body)

        @block.scalar
        def _(act):
            nc.scalar.preload_act_table(ACT.Gelu)

            def act_turn_x(b, kc):
                g, par = b.g + 1, (b.n + 1) % 2
                act.wait_ge(s_turnx, g * KC + kc + 1)
                if b.n >= 1:
                    act.wait_ge(s_z, (g - 1) * KC)
                    act.wait_ge(s_up, (g - 1) * NU)
                ps = spare[spare_at(TURN_X, kc) % 2]
                nc.scalar.activation(xq[:, par, kc, :], ps[:], ACT.Copy, scale=0.5).then_inc(s_xq, 1)
                nc.scalar.activation(xs[0][:, par, kc, :], ps[:], ACT.Copy, scale=0.5).then_inc(s_xhi, 1)

            def act_sigmoid(b):
                act.wait_ge(s_lg, b.g + 2)
                if b.n >= 0:
                    act.wait_ge(s_comb, b.g + 1)
                nc.scalar.activation(sg[:], lg[:], ACT.Sigmoid).then_inc(s_sg, 1)
                nc.scalar.preload_act_table(ACT.Gelu)

            def act_turn_g(b):
                act.wait_ge(s_turng, b.g + 2)
                if b.n >= 0:
                    act.wait_ge(s_sprps, (b.g + 1) * E)
                nc.scalar.activation(combt[:], gate_view(spare_at(TURN_G)), ACT.Copy).then_inc(s_combt, 1)

            def act_spread(b, e):
                act.wait_ge(s_sprps, (b.g + 1) * E + e + 1)
                if b.n >= 1:
                    act.wait_ge(s_prod, b.g * NU)
                nc.scalar.activation(spread[:, (b.n + 1) % 2, e, :], spare[spare_at(SPREAD, e) % 2][:],
                                     ACT.Copy).then_inc(s_spr, 1)

            def act_out(b, part):
                g = b.g - 1 - part
                act.wait_ge(s_turno, g * 2 + part + 1)
                if b.n - 1 - part >= 1:
                    act.wait_ge(s_out[part], 16 * TT * g)
                nc.scalar.activation(o_tok[:, part].rearrange("p j c -> p (j c)"),
                                     spare[spare_at(OUT, part) % 2][:], ACT.Copy).then_inc(s_otok, 1)

            def act_unit(b, u):
                kind, m = UNITS[u]
                act.wait_ge(s_up, b.g * NU + u + 1)
                if kind == EXPERT:
                    n = n_exp[u] - 1
                    if n >= NH:
                        act.wait_ge(s_prod, b.g * NU + n_exp.index(n - NH + 1) + 1)
                    elif b.n > 0:
                        act.wait_ge(s_prod, (b.g - 1) * NU + n_exp.index(NE + n - NH + 1) + 1)
                    nc.scalar.activation(act32[:, n % NH], up_ps[ring_at[u] % 2][:], ACT.Gelu,
                                         scale=1.0 / UP).then_inc(s_gelu, 1)
                else:
                    n = n_sha[u] - 1
                    if b.n > 0 or n >= 1:
                        act.wait_ge(s_su, b.g * NS + n)
                    nc.scalar.activation(half32[:], up_ps[ring_at[u] % 2][:], ACT.Tanh,
                                         scale=0.5 / UP).then_inc(s_tanh, 1)

            def act_high(b, back, u):
                g = b.g - back
                act.wait_ge(s_prod, g * NU + u + 1)
                if b.n - back > 0 or u >= NR:
                    act.wait_ge(s_down, g * NU + u - NR + 1)
                nc.scalar.activation(hid[0][:, u % NR], prod32[:, u % NH], ACT.Copy).then_inc(s_hi, 1)

            def act_z(b):
                act.wait_ge(s_z, b.g * KC)
                nc.scalar.activation(flat(zs[0][:]), flat(zq[:, (b.n - 1) % 2]), ACT.Copy
                                     ).then_inc(s_zhi, 1)

            def act_gate(b, s):
                r = b.g - 1
                act.wait_ge(s_step, r * TG + s + 1)
                nc.scalar.activation(th[:, s % 2].rearrange("p k b -> p (k b)"), gate_sums(s), ACT.Tanh,
                                     scale=0.5 / UP).then_inc(s_th, 1)

            def act_h(b, s):
                r = b.g - 1
                act.wait_ge(s_pre, r * TG + s + 1)
                if b.n > 1 and s in (0, HALF):
                    act.wait_ge(s_och, r * 2 if s else r * 2 - 1)
                src = flat3(pre[:, s % 2])
                nc.scalar.activation(flat3(hist[:, s]), src, ACT.Tanh).then_inc(s_h, 1)
                nc.scalar.activation(flat3(hs[0][:, s % 2]), src, ACT.Tanh).then_inc(s_hhi, 1)

            def spare_use(b, u):
                use = {TURN_X: act_turn_x, TURN_G: lambda b, _: act_turn_g(b), SPREAD: act_spread, OUT: act_out,
                       LOGITS: lambda b, _: None}
                for what, part, slot in SPARE:
                    if slot == u and b.there(what, part, b.n):
                        use[what](b, part)

            def body(b):
                for u in range(NU):
                    s = u - REC_SLOT
                    rec = b.tail and 0 <= s < TG
                    if rec:
                        act_gate(b, s)
                    if u > 0 and b.units:
                        act_high(b, 0, u - 1)
                    elif u == 0 and b.tail:
                        act_high(b, 1, NU - 1)
                    if rec:
                        act_h(b, s)
                    if b.units:
                        act_unit(b, u)
                    if u == 2 and b.tail:
                        act_z(b)
                    if u == SIGMOID_SLOT and b.prep:
                        act_sigmoid(b)
                    spare_use(b, u)

            def conv(n):
                _, dst, k, w = conv_parts(CONV[n])
                act.wait_ge(s_stage[n % NSTAGE], 16 * (n // NSTAGE + 1))
                nc.scalar.activation(dst[0], stage[:, n % NSTAGE, 0:k * w], ACT.Copy, scale=WUP
                                     ).then_inc(s_convhi, 1)

            act.wait_ge(s_condt, 1)
            prologue = Body(-1, -1)
            act_turn_x(prologue, 0)
            act_turn_x(prologue, 1)
            for n in range(4):
                conv(n)
            act_sigmoid(prologue)
            act_turn_g(prologue)
            for e in range(E):
                act_spread(prologue, e)
            for n in range(4, len(CONV)):
                conv(n)
            for i in range(2):
                act.wait_ge(s_turn0, i + 1)
                nc.scalar.activation(flat3(gwt[0][:, KC * i:KC * i + KC]), gate_ps[i][:], ACT.Copy,
                                     scale=(UP, WUP)[i]).then_inc(s_gwhi, 1)
            nc.scalar.activation(hist[:, TG - 1], cond_t[:, :, 0, :], ACT.Copy).then_inc(s_h, 1)
            nc.scalar.activation(hs[0][:, 1], cond_t[:, :, 0, :], ACT.Copy).then_inc(s_hhi, 1)
            run_bodies(act, body)

        @block.vector
        def _(dve):
            done = [0]

            def link(ins):
                done[0] += 1
                ins.then_inc(s_const, 1)
                dve.wait_ge(s_const, done[0])

            def low_x(b, kc):
                g, par = b.g + 1, (b.n + 1) % 2
                dve.wait_ge(s_xhi, g * KC + kc + 1)
                dve.tensor_tensor(xs[1][:, par, kc, :], xq[:, par, kc, :], xs[0][:, par, kc, :],
                                  ALU.subtract).then_inc(s_xlo, 1)

            def logits(b):
                g = b.g + 1
                dve.wait_ge(s_lgps, g + 1)
                if b.n >= 0:
                    dve.wait_ge(s_sg, g)
                dve.tensor_tensor(lg[:], spare[spare_at(LOGITS) % 2][:, 0:NJ * E].rearrange(
                    "p (j e) -> p j e", j=NJ), cond_lg[:], ALU.add).then_inc(s_lg, 1)

            R_STEPS = 10

            def route(b, first, last):
                g = b.g + 1
                def step(n, *ins):
                    if first <= n <= last:
                        if n > 0:
                            dve.wait_ge(s_route, g * R_STEPS + n)
                        elif b.n >= 0:
                            dve.wait_ge(s_turng, g)
                        for i in ins:
                            last_i = i()
                        if n < R_STEPS:
                            last_i.then_inc(s_route, 1)
                        else:
                            last_i.then_inc(s_comb, 1)

                if first == 0:
                    dve.wait_ge(s_sg, g + 1)
                step(0, lambda: dve.tensor_tensor(sel[:, :, 0:E], sg[:], rbias[:], ALU.add))
                step(1, lambda: dve.memset(fence[:], 0.0), *[(lambda j=j: dve.max(top8[:, j], sel[:, j, 0:E])) for j in range(NJ)])
                step(2, lambda: dve.tensor_copy(seek[:, :, 0:TOPK], top8[:, :, 0:TOPK]))
                step(3, lambda: dve.memset(fence[:], 0.0), *[(lambda j=j: dve.match_replace(left[:, j], seek[:, j], sel[:, j], TAKEN))
                          for j in range(NJ)])
                step(4, lambda: dve.tensor_tensor(mask[:], left[:, :, 0:E], sel[:, :, 0:E], ALU.not_equal))
                step(5, lambda: dve.tensor_tensor(smask[:], mask[:], sg[:], ALU.mult))
                step(6, lambda: dve.tensor_reduce(den[:], smask[:], AX_X, ALU.add))
                step(7, lambda: dve.tensor_scalar(deps[:], den[:], 1e-9, None, ALU.add),
                     lambda: dve.tensor_scalar(okay[:], den[:], 1e-9, None, ALU.is_gt))
                step(8, lambda: dve.reciprocal(drec[:], deps[:]),
                     lambda: dve.tensor_scalar(alt[:], okay[:], -1.0 / TOPK, 1.0 / TOPK, ALU.mult, ALU.add))
                step(9, lambda: dve.tensor_tensor(part_b[:], mask[:], bcast(alt), ALU.mult),
                     lambda: dve.tensor_tensor(okrec[:], drec[:], okay[:], ALU.mult))
                step(10, lambda: gates_end(g))

            def gates_end(g):
                dve.tensor_tensor(part_a[:], smask[:], bcast(okrec), ALU.mult).then_inc(s_gates, 1)
                dve.wait_ge(s_gates, g * 3 + 1)
                dve.tensor_tensor(comb[:], part_a[:], part_b[:], ALU.add).then_inc(s_gates, 1)
                dve.wait_ge(s_gates, g * 3 + 2)
                dve.tensor_copy(comb16[:, :, 0, :], comb[:]).then_inc(s_gates, 1)
                dve.wait_ge(s_gates, g * 3 + 3)
                return dve.tensor_tensor(comb16[:, :, 1, :], comb[:], comb16[:, :, 0, :], ALU.subtract)

            def product(b, u):
                kind, m = UNITS[u]
                if b.n > 0 or u >= NH:
                    dve.wait_ge(s_lo, b.g * NU + u - NH + 1)
                    dve.wait_ge(s_hi, b.g * NU + u - NH + 1)
                if kind == EXPERT:
                    n = n_exp[u] - 1
                    dve.wait_ge(s_gelu, b.g * NE + n + 1)
                    if m == 0:
                        dve.wait_ge(s_spr, b.g * E + E)
                    dve.tensor_tensor(prod32[:, u % NH], act32[:, n % NH], spread[:, b.n % 2, m // 2, :],
                                      ALU.mult).then_inc(s_prod, 1)
                else:
                    n = n_sha[u] - 1
                    r = ring_at[u]
                    dve.wait_ge(s_tanh, b.g * NS + n + 1)
                    dve.scalar_tensor_tensor(prod32[:, u % NH], half32[:], 1.0, up_ps[r % 2][:],
                                             ALU.add, ALU.mult).then_inc(s_su, 1)
                    dve.wait_ge(s_su, b.g * NS + n + 1)
                    dve.scalar_tensor_tensor(prod32[:, u % NH], prod32[:, u % NH], 0.5 / (UP * UP),
                                             up_ps[(r + 1) % 2][:], ALU.mult, ALU.mult).then_inc(s_prod, 1)

            def low(b, back, u):
                g = b.g - back
                dve.wait_ge(s_hi, g * NU + u + 1)
                if b.n - back > 0 or u >= NR:
                    dve.wait_ge(s_down, g * NU + u - NR + 1)
                dve.tensor_tensor(hid[1][:, u % NR], prod32[:, u % NH], hid[0][:, u % NR], ALU.subtract
                                  ).then_inc(s_lo, 1)

            def residual(b):
                par = (b.n - 1) % 2
                dve.wait_ge(s_down, b.g * NU)
                if b.n >= 3:
                    dve.wait_ge(s_och, (b.g - 3) * 2 + 2)
                for kc in range(KC):
                    dve.scalar_tensor_tensor(zq[:, par, :, kc, :],
                                             y_ps[kc][:].rearrange("p (t b) -> p t b", b=NB), MEAN,
                                             xq[:, par, kc, :].rearrange("p (t b) -> p t b", b=NB),
                                             ALU.mult, ALU.add).then_inc(s_z, 1)

            def low_z(b):
                dve.wait_ge(s_zhi, b.g)
                dve.tensor_tensor(flat(zs[1][:]), flat(zq[:, (b.n - 1) % 2]), flat(zs[0][:]), ALU.subtract
                                  ).then_inc(s_zlo, 1)

            def rec_pre(b, s):
                r = b.g - 1
                z = zq[:, (b.n - 1) % 2, s]
                dve.wait_ge(s_th, r * TG + s + 1)
                dve.scalar_tensor_tensor(flat3(gz[:]), flat3(th[:, s % 2]), 1.0, flat3(z), ALU.add, ALU.mult
                                         ).then_inc(s_gz, 1)
                dve.wait_ge(s_gz, r * TG + s + 1)
                dve.wait_ge(s_hl, r * TG + s + 1)
                dve.tensor_tensor(flat3(pre[:, s % 2]), flat3(gz[:]), flat3(hl[:, s % 2]), ALU.add
                                  ).then_inc(s_pre, 1)

            def rec_low(b, s):
                r = b.g - 1
                dve.wait_ge(s_hhi, r * TG + s + 2)
                dve.tensor_tensor(flat3(hs[1][:, s % 2]), flat3(hist[:, s]), flat3(hs[0][:, s % 2]),
                                  ALU.subtract).then_inc(s_hlo, 1)

            def out_channels(b, part):
                g = b.g - 1 - part
                par = (b.n - 1 - part) % 2
                if part == 1 or b.n > 1:
                    dve.wait_ge(s_turno, g * 2 + part)
                if part == 1:
                    dve.wait_ge(s_h, (g + 1) * TG + 1)
                else:
                    dve.wait_ge(s_h, g * TG + HALF + 1)
                for kc in range(KC):
                    ins = dve.scalar_tensor_tensor(o_ch[:, kc], zq[:, par, part * HALF:(part + 1) * HALF, kc, :],
                                                   2.0, hist[:, part * HALF:(part + 1) * HALF, kc, :],
                                                   ALU.mult, ALU.add)
                ins.then_inc(s_och, 1)

            def body(b):
                for u in range(NU):
                    s = u - REC_SLOT
                    rec = b.tail and 0 <= s < TG
                    if u == 0 and b.late:
                        out_channels(b, 1)
                    if rec:
                        rec_pre(b, s)
                    if u > 0 and b.units:
                        low(b, 0, u - 1)
                    elif u == 0 and b.tail:
                        low(b, 1, NU - 1)
                    if rec:
                        rec_low(b, s)
                    if u == 2 and b.tail:
                        residual(b)
                    if u == 3 and b.tail:
                        low_z(b)
                    if b.units:
                        product(b, u)
                    if b.prep:
                        for what, part, slot in SPARE:
                            if what == TURN_X and slot == u:
                                low_x(b, part)
                        if u == SIGMOID_SLOT:
                            logits(b)
                        if u == ROUTE_SLOT:
                            route(b, 0, 5)
                        if u == ROUTE_SLOT + 1:
                            route(b, 6, R_STEPS)
                    if u == REC_SLOT + HALF and b.tail:
                        out_channels(b, 0)

            def conv(n):
                _, dst, k, w = conv_parts(CONV[n])
                dve.wait_ge(s_convhi, n + 1)
                dve.scalar_tensor_tensor(dst[1], stage[:, n % NSTAGE, 0:k * w], WUP, dst[0],
                                         ALU.mult, ALU.subtract).then_inc(s_conv, 1)

            link(dve.memset(ones[:], 1.0))
            link(dve.memset(ones2[:], 1.0))
            link(dve.memset(sel[:], PAD))
            link(dve.memset(seek[:], PAD))
            dve.wait_ge(s_ident, 2)
            link(dve.tensor_copy(ident16[:], ident[:]))
            link(dve.tensor_tensor(pick2[:], ident[0:16, 0:E], ident[0:16, E:2 * E], ALU.add))
            for e in range(E):
                link(dve.tensor_scalar(pick[:, e, :], ones[0:16, :], pick2[:, e:e + 1], None, ALU.mult))
            dve.wait_ge(s_clg_ps, 1)
            for t in range(TT):
                ins = dve.tensor_copy(cond_t[:, :, t, :], bank[0][:, 0:STEP].rearrange("p (k b) -> p k b", k=KC))
            ins.then_inc(s_condt, 1)
            dve.wait_ge(s_rw, 16)
            dve.wait_ge(s_small, 16 * SMALL)
            link(dve.tensor_scalar(rwx[:], rw[:, 0:KC, :], 2.0, None, ALU.mult))
            dve.wait_ge(s_clg_ps, 2)
            link(dve.tensor_copy(cond_lg[:, 0, :], bank[1][:, 0:E]))
            for j in range(1, NJ):
                link(dve.tensor_copy(cond_lg[:, j, :], cond_lg[:, 0, :]))
            link(dve.tensor_scalar(al1[:], al[:], -1.0, 1.0, ALU.mult, ALU.add))
            for kc in range(KC):
                link(dve.tensor_scalar(leak[:, kc, :], ones[:, 0:NB], al1[:, kc:kc + 1], None, ALU.mult))
            link(dve.tensor_scalar(gb_full[:], gb_in[:], UP, None, ALU.mult))
            link(dve.tensor_copy(gb_hi[:], gb_full[:]))
            link(dve.tensor_tensor(gb_lo[:], gb_full[:], gb_hi[:], ALU.subtract))
            link(dve.tensor_scalar(gb_lo2[:], gb_lo[:], ident[0:2, 1:2], None, ALU.mult))
            link(dve.scalar_tensor_tensor(gb[:], gb_hi[:], ident[0:2, 0:1], gb_lo2[:], ALU.mult, ALU.add))
            assert done[0] == N_CONST
            prologue = Body(-1, -1)
            low_x(prologue, 0)
            low_x(prologue, 1)
            logits(prologue)
            for n in range(4):
                conv(n)
            route(prologue, 0, R_STEPS)
            for n in range(4, len(CONV)):
                conv(n)
            for i in range(2):
                dve.wait_ge(s_gwhi, i + 1)
                dve.scalar_tensor_tensor(flat3(gwt[1][:, KC * i:KC * i + KC]), gate_ps[i][:], (UP, WUP)[i],
                                         flat3(gwt[0][:, KC * i:KC * i + KC]), ALU.mult, ALU.subtract
                                         ).then_inc(s_gwlo, 1)
            dve.wait_ge(s_hhi, 1)
            dve.tensor_tensor(flat3(hs[1][:, 1]), flat3(hist[:, TG - 1]), flat3(hs[0][:, 1]),
                              ALU.subtract).then_inc(s_hlo, 1)
            run_bodies(dve, body)

        @block.tensor
        def _(pe):
            def pairs(out_ap, w, mov, start, stop, chunks):
                last, n = None, len(chunks) * 3
                for i, k in enumerate(chunks):
                    for j, (a, c) in enumerate(((0, 0), (1, 0), (0, 1))):
                        last = pe.matmul(out_ap, w(a, k), mov(c, k), start=start and i == 0 and j == 0,
                                         stop=stop and i * 3 + j == n - 1, skip_group_check=True)
                return last

            def up(b, u):
                kind, m = UNITS[u]
                par = b.n % 2
                r = ring_at[u]

                def free(slot):
                    before = slot - 2
                    back = 0
                    if before < 0:
                        before, back = before + at, 1
                    if b.n - back < 0:
                        return
                    v = max(i for i in range(NU) if ring_at[i] <= before)
                    if UNITS[v][0] == EXPERT:
                        pe.wait_ge(s_gelu, (b.g - back) * NE + n_exp[v])
                    elif before == ring_at[v] + 1:
                        pe.wait_ge(s_prod, (b.g - back) * NU + v + 1)
                    else:
                        pe.wait_ge(s_su, (b.g - back) * NS + n_sha[v])

                mov = lambda c, k: xs[c][:, par, k, :]
                if u == 0:
                    pe.wait_ge(s_xlo, b.g * KC + KC)
                if kind == EXPERT:
                    e, h = m // 2, m % 2
                    conv_ready(pe, b.n, ("w1e", e))
                    free(r)
                    pairs(up_ps[r % 2][:], lambda a, k: w1e_s[a][:, e, k, h * P:(h + 1) * P], mov,
                          True, True, range(KC)).then_inc(s_up, 1)
                else:
                    for i in range(2):
                        conv_ready(pe, b.n, ("w13", i))
                        free(r + i)
                        last = pairs(up_ps[(r + i) % 2][:], lambda a, k: w13_s[a][:, i, k, m * P:(m + 1) * P],
                                     mov, True, True, range(KC))
                    last.then_inc(s_up, 1)

            def down(b, back, u):
                kind, m = UNITS[u]
                g = b.g - back
                e, h = m // 2, m % 2
                conv_ready(pe, b.n - back, ("w2e", e) if kind == EXPERT else ("w2", 0))
                if u == 0 and b.n - back > 0:
                    pe.wait_ge(s_z, g * KC)
                pe.wait_ge(s_lo, g * NU + u + 1)
                for kc in range(KC):
                    cols = slice(kc * P, (kc + 1) * P)
                    last = pairs(y_ps[kc][:],
                                 lambda a, k: (w2e_s[a][:, e, h, cols] if kind == EXPERT else w2_s[a][:, m, cols]),
                                 lambda c, k: hid[c][:, u % NR], u == 0, u == NU - 1, [0])
                last.then_inc(s_down, 1)

            def gate_fill(b):
                pe.wait_ge(s_zlo, b.g)
                for hf in range(2):
                    if b.n > 1:
                        pe.wait_ge(s_th, (b.g - 1) * TG if hf else (b.g - 1) * TG - HALF)
                    for jc in range(KC):
                        cols = slice(jc * P, (jc + 1) * P)
                        dst = gate_ps[hf][:].rearrange("p (t k b) -> p t k b", k=KC, b=NB)[:, :, jc, :]
                        pe.matmul(dst, gb[:, cols], ones2[:].rearrange("p (t b) -> p t b", b=NB),
                                  start=jc == 0, stop=False, skip_group_check=True)
                        pairs(dst, lambda a, k: gwt[a][:, KC + k, cols],
                              lambda c, k: zs[c][:, hf * HALF:(hf + 1) * HALF, k, :], False, False, range(KC))

            def gate_step(b, s):
                r = b.g - 1
                for c, weights, ready in ((0, (0, 1), s_hhi), (1, (0,), s_hlo)):
                    pe.wait_ge(ready, r * TG + s + 1)
                    for jc in range(KC):
                        for a in weights:
                            for k in range(KC):
                                last = pe.matmul(gate_sums(s)[:, jc * NB:(jc + 1) * NB], gwt[a][:, k, jc * P:(jc + 1) * P],
                                                 hs[c][:, (s - 1) % 2, k, :], start=False, stop=False,
                                                 skip_group_check=True)
                last.then_inc(s_step, 1)

            def spare_use(b, pos):
                what, part, _ = SPARE[pos]
                if not b.there(what, part, b.n):
                    return
                ps = spare[pos % 2]
                released(pe, b, pos)
                if what == TURN_X:
                    g, par = b.g + 1, (b.n + 1) % 2
                    if part == 0:
                        pe.wait_ge(s_x[par], b.loads * (16 * TT))
                    for j in range(NJ):
                        last = pe.transpose(ps[:, j * P:(j + 1) * P], x_tok[:, par, j, part * P:(part + 1) * P],
                                            ident[:])
                    last.then_inc(s_turnx, 1)
                elif what == LOGITS:
                    g, par = b.g + 1, (b.n + 1) % 2
                    pe.wait_ge(s_xq, g * KC + KC)
                    for j in range(NJ):
                        for k in range(KC):
                            last = pe.matmul(ps[:, j * E:(j + 1) * E], xq[:, par, k, j * P:(j + 1) * P],
                                             rwx[:, k, :], start=k == 0, stop=k == KC - 1)
                    last.then_inc(s_lgps, 1)
                elif what == TURN_G:
                    pe.wait_ge(s_comb, b.g + 2)
                    view = gate_view(pos)
                    for j in range(NJ):
                        last = pe.transpose(view[:, j * P:(j + 1) * P],
                                            comb16[:, j].rearrange("p a e -> p (a e)"), ident16[:])
                    last.then_inc(s_turng, 1)
                elif what == SPREAD:
                    pe.wait_ge(s_combt, b.g + 2)
                    pe.matmul(ps[:], pick[:, part, :], combt[:], start=True, stop=True).then_inc(s_sprps, 1)
                else:
                    g = b.g - 1 - part
                    pe.wait_ge(s_och, g * 2 + part + 1)
                    for j in range(NJ // 2):
                        for kc in range(KC):
                            last = pe.transpose(ps[:, j * C + kc * P:j * C + (kc + 1) * P],
                                                o_ch[:, kc, j * TT:(j + 1) * TT, :].rearrange("p t b -> p (t b)"),
                                                ident[:])
                    last.then_inc(s_turno, 1)

            def body(b):
                for u in range(NU):
                    if b.units:
                        up(b, u)
                    if u == 3 and b.tail:
                        gate_fill(b)
                    s = u - REC_SLOT
                    if b.tail and 0 <= s < TG:
                        gate_step(b, s)
                    if u < DOWN_LAG:
                        if b.tail:
                            down(b, 1, NU - DOWN_LAG + u)
                    elif b.units:
                        down(b, 0, u - DOWN_LAG)
                    for pos, (what, part, slot) in enumerate(SPARE):
                        if slot == u:
                            spare_use(b, pos)

            pe.wait_ge(s_ident, 2)
            pe.wait_ge(s_cond, 16)
            for k in range(KC):
                last = pe.transpose(bank[0][:, k * NB:(k + 1) * NB], cond_in[:, k * P:(k + 1) * P],
                                    ident[0:NB, 0:NB])
            last.then_inc(s_clg_ps, 1)
            prologue = Body(-1, -1)
            PROLOGUE = [p for p, u in enumerate(SPARE) if u[0] != OUT]
            spare_use(prologue, PROLOGUE[0])
            spare_use(prologue, PROLOGUE[1])
            pe.wait_ge(s_condt, 1)
            pe.wait_ge(s_rw, 16)
            for k in range(KC):
                last = pe.matmul(bank[1][:, 0:E], cond_t[:, k].rearrange("p t b -> p (t b)"), rw[:, KC + k, :],
                                 start=k == 0, stop=k == KC - 1)
            last.then_inc(s_clg_ps, 1)
            pe.wait_ge(s_const, N_CONST)
            for p in PROLOGUE[2:]:
                spare_use(prologue, p)
            pe.wait_ge(s_gw, 16)
            for i in range(2):
                for k in range(KC):
                    for jc in range(KC):
                        c0 = (i * KC + k) * P
                        last = pe.transpose(gate_ps[i][:, k * C + jc * P:k * C + (jc + 1) * P],
                                            gw[:, jc, c0:c0 + P], ident[:])
                last.then_inc(s_turn0, 1)
            pe.wait_ge(s_h, 1)
            pe.wait_ge(s_gwlo, 2)
            run_bodies(pe, body)


_INS = ['x', 'cond_1024', 'L0_cond_router_W', 'L0_cond_router_bias', 'L0_cond_w1', 'L0_cond_w3', 'L0_cond_w2',
        'L0_cond_W1e', 'L0_cond_W2e', 'L1_cond_W', 'L1_cond_b', 'L1_cond_alpha']
_OUTS = [((32, 256, 256), 'float32')]


def kernel(**inputs):
    import numpy as _np
    import concourse.bacc as _bacc
    from concourse import mybir as _mybir
    from concourse.bass_utils import run_bass_kernel_spmd as _run

    nc = _bacc.Bacc("TRN2", target_bir_lowering=False, num_devices=1)
    arrays, args = {}, []
    for name in _INS:
        a = _np.ascontiguousarray(inputs[name])
        arrays[f"in_{name}_dram"] = a
        args.append(nc.dram_tensor(f"in_{name}_dram", a.shape, _mybir.dt.from_np(a.dtype), kind="ExternalInput").ap())
    for i, (shape, dtype) in enumerate(_OUTS):
        dt = _mybir.dt.from_np(_np.dtype(dtype))
        args.append(nc.dram_tensor(f"out_{i}_dram", shape, dt, kind="ExternalOutput").ap())
    moe_gated_recurrence(nc, *args)
    r = _run(nc, [arrays], core_ids=[0])
    got = tuple(r.results[0][f"out_{i}_dram"] for i in range(len(_OUTS)))
    return got[0]
```

```python
from contextlib import ExitStack

import concourse.bass as bass
from concourse import mybir

F32 = mybir.dt.float32
F16 = mybir.dt.float16
ALU = mybir.AluOpType
ACT = mybir.ActivationFunctionType
AX_X = mybir.AxisListType.X

P = 128
TOPK = 2
N_SHARED = 1

EXPERT, SHARED = "expert", "shared"
UNITS = []
for _n in range(4):
    UNITS += [(EXPERT, 4 * _n), (EXPERT, 4 * _n + 1), (SHARED, _n), (EXPERT, 4 * _n + 2), (EXPERT, 4 * _n + 3)]
NU = len(UNITS)
SETUP_SLOT = NU - 3
DOWN_LAG = 2
REC_SLOT = 4

TURN_X, OUT, LOGITS, TURN_G = "turn_x", "out", "logits", "turn_g"
SPARE = [(OUT, 1, 3), (TURN_X, 0, 6), (TURN_X, 1, 8), (LOGITS, 0, 10), (OUT, 0, 12), (TURN_G, 0, 15)]
SIGMOID_SLOT = 11
ROUTE_SLOT = 12

TAKEN = 3.0e38
PAD = -3.0e38
N_CONST = 15
N_ROUTER_CONST = 4


def moe_gated_recurrence(nc, x, cond, router_w, router_b, w1, w3, w2, w1e, w2e, gate_w, gate_b, alpha, out):
    NB, T, C = x.shape
    E, _, HE = w1e.shape
    HS = w1.shape[1]
    SMALL = 3
    KC = C // P
    TT = P // NB
    NJ = 4
    TG = NJ * TT
    G = NJ * P
    NG = T // TG
    HALF = TG // 2
    STEP = KC * NB
    MID = HS // P
    assert KC == 2 and HE == 2 * P and MID == 4 and E == 8 and NG == 16
    assert sum(k == EXPERT for k, _ in UNITS) == E * HE // P

    WUP = 64.0
    UP = 0.5 * WUP
    WDN = 64.0
    MEAN = 0.5 / ((N_SHARED + TOPK) * WDN)

    gates_dram = nc.dram_tensor("gates_by_expert", [2, E * G], F32).ap()
    x_in = x.rearrange("b (g j t) c -> g t b j c", j=NJ, t=TT)
    out_v = out.rearrange("b (g h j t) c -> g h t b j c", h=2, j=NJ // 2, t=TT)

    with ExitStack() as ctx:
        def sb(name, shape, dt=F32):
            return ctx.enter_context(nc.sbuf_tensor(name, shape, dt))

        def sem(name):
            return ctx.enter_context(nc.semaphore(name))

        bank = [ctx.enter_context(nc.psum_tensor(f"bank{i}", [P, 512], F32)) for i in range(8)]
        RING = 3
        up_ps = bank[0:RING]
        y_ps = bank[3:5]
        gate_ps = bank[5:7]
        spare = bank[7]

        NSTAGE = 8
        stage = sb("stage", [P, NSTAGE, 1024])
        w1e_s = [sb(f"w1e_{h}", [P, E, KC, HE], F16) for h in ("high", "low")]
        w2e_s = [sb(f"w2e_{h}", [P, E, KC, C], F16) for h in ("high", "low")]
        w13_s = [sb(f"w13_{h}", [P, 2, KC, HS], F16) for h in ("high", "low")]
        w2_s = [sb(f"w2_{h}", [P, MID, C], F16) for h in ("high", "low")]
        gw = sb("gw", [P, KC, 2 * C])
        gwt = [sb(f"gwt_{h}", [P, 2 * KC, C], F16) for h in ("high", "low")]
        rw = sb("rw", [P, 2 * KC, E])
        rwx = [sb(f"rwx_{h}", [P, KC, E], F16) for h in ("high", "low")]
        gb_in = sb("gb_in", [2, C])
        gb_full = sb("gb_full", [2, C])
        gb_hi = sb("gb_hi", [2, C], F16)
        gb_lo = sb("gb_lo", [2, C], F16)
        gb_lo2 = sb("gb_lo2", [2, C], F16)
        gb = sb("gb", [2, C], F16)
        ones2 = sb("ones2", [2, HALF * NB], F16)
        al = sb("al", [P, KC])
        al1 = sb("al1", [P, KC])
        ones = sb("ones", [P, P])
        leak = sb("leak", [P, KC, NB])
        ident = sb("ident", [P, P])
        cond_in = sb("cond_in", [NB, C])
        cond_t = sb("cond_t", [P, KC, TT, NB])
        cond_lg = sb("cond_lg", [P, E])
        rbias = sb("rbias", [P, E])

        x_tok = sb("x_tok", [P, 2, NJ, C])
        xq = sb("xq", [P, 2, KC, G])
        xs = [sb(f"xs_{h}", [P, 2, KC, G], F16) for h in ("high", "low")]
        lg = sb("lg", [P, NJ, E])
        sg = sb("sg", [P, NJ, E])
        sel = sb("sel", [P, NJ, 16])
        top8 = sb("top8", [P, NJ, 8])
        seek = sb("seek", [P, NJ, 8])
        left = sb("left", [P, NJ, 16])
        fence = sb("fence", [P, 1])
        mask = sb("mask", [P, NJ, E])
        smask = sb("smask", [P, NJ, E])
        den = sb("den", [P, NJ])
        deps = sb("deps", [P, NJ])
        drec = sb("drec", [P, NJ])
        okay = sb("okay", [P, NJ])
        okrec = sb("okrec", [P, NJ])
        alt = sb("alt", [P, NJ])
        part_a = sb("part_a", [P, NJ, E])
        part_b = sb("part_b", [P, NJ, E])
        comb = sb("comb", [P, NJ, E])
        combt = sb("combt", [E, G])
        spread = sb("spread", [P, 2, E, G])
        NH, NR = 2, 4
        act32 = sb("act32", [P, NH, G])
        half32 = sb("half32", [P, G])
        prod32 = sb("prod32", [P, NH, G])
        hid = [sb(f"hid_{h}", [P, NR, G], F16) for h in ("high", "low")]
        zq = sb("zq", [P, 2, TG, KC, NB])
        zs = [sb(f"zs_{h}", [P, TG, KC, NB], F16) for h in ("high", "low")]
        hist = sb("hist", [P, TG, KC, NB])
        hs = [sb(f"hs_{h}", [P, 2, KC, NB], F16) for h in ("high", "low")]
        th = sb("th", [P, 2, KC, NB])
        gz = sb("gz", [P, KC, NB])
        pre = sb("pre", [P, 2, KC, NB])
        hl = sb("hl", [P, 2, KC, NB])
        o_ch = sb("o_ch", [P, KC, HALF, NB])
        o_tok = sb("o_tok", [P, 2, 2, C])

        s_x = [sem("s_x_even"), sem("s_x_odd")]
        s_rw = sem("s_rw")
        s_small = sem("s_small")
        s_rbias = sem("s_rbias")
        s_cond = sem("s_cond")
        s_gw = sem("s_gw")
        s_stage = [sem(f"s_stage{i}") for i in range(NSTAGE)]
        s_ident = sem("s_ident")
        s_const = sem("s_const")
        s_convhi = sem("s_convhi")
        s_conv = sem("s_conv")
        s_turn0 = sem("s_turn0")
        s_gwhi = sem("s_gwhi")
        s_gwlo = sem("s_gwlo")
        s_condt = sem("s_condt")
        s_clg_ps = sem("s_clg_ps")
        s_up = sem("s_up")
        s_gelu = sem("s_gelu")
        s_tanh = sem("s_tanh")
        s_su = sem("s_su")
        s_prod = sem("s_prod")
        s_hi = sem("s_hi")
        s_lo = sem("s_lo")
        s_down = sem("s_down")
        s_z = sem("s_z")
        s_zhi = sem("s_zhi")
        s_zlo = sem("s_zlo")
        s_step = sem("s_step")
        s_th = sem("s_th")
        s_gz = sem("s_gz")
        s_pre = sem("s_pre")
        s_h = sem("s_h")
        s_hhi = sem("s_hhi")
        s_hlo = sem("s_hlo")
        s_hl = sem("s_hl")
        s_turnx = sem("s_turnx")
        s_xq = sem("s_xq")
        s_xhi = sem("s_xhi")
        s_xlo = sem("s_xlo")
        s_lgps = sem("s_lgps")
        s_lg = sem("s_lg")
        s_sg = sem("s_sg")
        s_route = sem("s_route")
        s_gates = sem("s_gates")
        s_comb = sem("s_comb")
        s_turng = sem("s_turng")
        s_combt = sem("s_combt")
        s_gdram = sem("s_gdram")
        s_spr = [sem("s_spr_even"), sem("s_spr_odd")]
        s_spr_first = sem("s_spr_first")
        s_och = sem("s_och")
        s_turno = sem("s_turno")
        s_otok = sem("s_otok")
        s_out = [sem("s_out_first"), sem("s_out_second")]

        class Body:
            def __init__(self, g, n, loads=None):
                self.g, self.n = g, n
                self.loads = (n + 1) // 2 + 1 if loads is None else loads
                self.spreads = n // 2 + 1 if loads is None else loads - n % 2
                self.units = n < NG
                self.tail = 1 <= n <= NG
                self.prep = n + 1 < NG
                self.late = 2 <= n <= NG + 1

            def there(self, what, part, n):
                if what == OUT:
                    return (1 <= n <= NG) if part == 0 else (2 <= n <= NG + 1)
                return 0 <= n + 1 < NG

        def released(eng, body, pos):
            p, back = pos - 1, 0
            while p < 0 or not body.there(*SPARE[p][0:2], body.n - back):
                p -= 1
                if p < 0:
                    p += len(SPARE)
                    back += 1
                if body.n - back < -1:
                    return
            what, part, _ = SPARE[p]
            g = (body.g - back - 1 - part) if what == OUT else (body.g - back + 1)
            if what == TURN_X:
                eng.wait_ge(s_xhi, g * KC + part + 1)
            elif what == OUT:
                eng.wait_ge(s_otok, g * 2 + part + 1)
            elif what == LOGITS:
                eng.wait_ge(s_lg, g + 1)
            else:
                eng.wait_ge(s_combt, g + 1)

        ring_at, at = [], 0
        for kind, _ in UNITS:
            ring_at.append(at)
            at += 1 if kind == EXPERT else 2
        assert at % RING == 0
        n_exp = [sum(k == EXPERT for k, _ in UNITS[:u + 1]) for u in range(NU)]
        n_sha = [sum(k == SHARED for k, _ in UNITS[:u + 1]) for u in range(NU)]
        NE, NS = n_exp[-1], n_sha[-1]

        CONV, CONV_SLOT = [], []
        for u, (kind, m) in enumerate(UNITS):
            keys = [("w1e", m // 2), ("w2e", m // 2)] if kind == EXPERT else [("w13", 0), ("w13", 1), ("w2", 0)]
            for key in keys:
                if key not in CONV:
                    CONV.append(key)
                    CONV_SLOT.append(max(u - 3, -1))
        CONV_AT = {key: n for n, key in enumerate(CONV)}

        def conv_parts(key):
            kind, i = key
            if kind == "w1e":
                src, dst = w1e[i].rearrange("(k p) h -> p k h", p=P), [w[:, i] for w in w1e_s]
            elif kind == "w2e":
                src, dst = w2e[i].rearrange("(k p) h -> p k h", p=P), [w[:, i] for w in w2e_s]
            elif kind == "w13":
                src, dst = (w1, w3)[i].rearrange("(k p) h -> p k h", p=P), [w[:, i] for w in w13_s]
            else:
                src, dst = w2.rearrange("(k p) h -> p k h", p=P), [w[:, :, :] for w in w2_s]
            k, w = src.shape[1], src.shape[2]
            return src, [d.rearrange("p k h -> p (k h)") for d in dst], k, w

        def conv_ready(eng, n, key):
            if n == 0:
                eng.wait_ge(s_conv, CONV_AT[key] + 1)

        def run_bodies(eng, body):
            for n in range(3):
                body(Body(n, n))
            with eng.Fori(1, NG // 2 - 1) as i:
                body(Body(i * 2 + 1, 3, i + 2))
                body(Body(i * 2 + 2, 4, i + 2))
            for n in range(NG - 1, NG + 2):
                body(Body(n, n))

        def bcast(ap):
            return ap[:].rearrange("p (j a) -> p j a", a=1).broadcast_to([P, NJ, E])

        def every_tile(ap):
            return ap[:].rearrange("p (a e) -> p a e", a=1).broadcast_to([P, NJ, E])

        def flat(ap):
            return ap.rearrange("p t k b -> p (t k b)")

        def flat3(ap):
            return ap.rearrange("p k b -> p (k b)")

        def gate_sums(s):
            at_col = (s % HALF) * STEP
            return gate_ps[s // HALF][:, at_col:at_col + STEP]


        block = ctx.enter_context(nc.Block())

        @block.sync
        def _(sp):
            def load_x(g, par):
                for t in range(TT):
                    sp.dma_start(x_tok[NB * t:NB * (t + 1), par, :, :], x_in[g, t]).then_inc(s_x[par], 16)

            def load_weight(n):
                src, _, k, w = conv_parts(CONV[n])
                if n >= NSTAGE:
                    sp.wait_ge(s_conv, n - NSTAGE + 1)
                sp.dma_start(stage[:, n % NSTAGE, 0:k * w].rearrange("p (k w) -> p k w", k=k),
                             src).then_inc(s_stage[n % NSTAGE], 16)

            def body(b):
                if b.prep and b.n >= 1:
                    sp.wait_ge(s_turnx, b.g * KC)
                    load_x(b.g + 1, (b.n + 1) % 2)
                for part, there, g in ((1, b.late, b.g - 2), (0, b.tail, b.g - 1)):
                    if there:
                        sp.wait_ge(s_otok, g * 2 + part + 1)
                        for t in range(TT):
                            sp.dma_start(out_v[g, part, t], o_tok[NB * t:NB * (t + 1), part, :, :]
                                         ).then_inc(s_out[part], 16)
                if b.prep:
                    spread_gates(b)

            def spread_gates(b):
                g, par = b.g + 1, (b.n + 1) % 2
                sp.wait_ge(s_combt, g + 1)
                sp.dma_start(gates_dram[par].rearrange("(e g) -> e g", e=E), combt[:]).then_inc(s_gdram, 16)
                sp.wait_ge(s_gdram, (g + 1) * 16)
                cuts = (0, E * G) if b.n >= 0 else (0, 2 * G, E * G)
                for lo, hi in zip(cuts, cuts[1:]):
                    sp.dma_start(spread[:, par].rearrange("p e g -> p (e g)")[:, lo:hi],
                                 gates_dram[par:par + 1, lo:hi].broadcast_to([P, hi - lo])
                                 ).then_inc(s_spr[par] if hi == E * G else s_spr_first, 16)

            load_x(0, 0)
            for n in range(NSTAGE):
                load_weight(n)
            load_x(1, 1)
            spread_gates(Body(-1, -1))
            for k in range(KC):
                sp.dma_start(al[:, k:k + 1], alpha.rearrange("(k p a) -> k p a", p=P, a=1)[k]).then_inc(s_small, 16)
            sp.dma_start(gb_in[:], gate_b.rearrange("(a c) -> a c", a=1).broadcast_to([2, C])
                         ).then_inc(s_small, 16)
            for n in range(NSTAGE, len(CONV)):
                load_weight(n)
            sp.dma_start(gw[:], gate_w.rearrange("(k p) c -> p k c", p=P)).then_inc(s_gw, 16)
            run_bodies(sp, body)
            for part in range(2):
                sp.wait_ge(s_out[part], 16 * TT * NG)

        @block.gpsimd
        def _(pool):
            nc.gpsimd.memset(ident[:], 0.0).then_inc(s_ident, 1)
            pool.wait_ge(s_ident, 1)
            nc.gpsimd.affine_select(out=ident[:], in_=ident[:], compare_op=ALU.not_equal, fill=1.0,
                                    base=0, pattern=[[-1, P]], channel_multiplier=1).then_inc(s_ident, 1)

            def body(b):
                if not b.tail:
                    return
                for s in range(TG):
                    pool.wait_ge(s_h, (b.g - 1) * TG + s + 1)
                    nc.gpsimd.tensor_tensor(hl[:, s % 2], hist[:, (s - 1) % TG], leak[:], ALU.mult
                                            ).then_inc(s_hl, 1)

            pool.wait_ge(s_const, N_CONST)
            run_bodies(pool, body)

        @block.scalar
        def _(act):
            act.dma_start(cond_in[:], cond).then_inc(s_cond, 16)
            act.dma_start(rw[:], router_w.rearrange("(k p) e -> p k e", p=P)).then_inc(s_rw, 16)
            nc.scalar.preload_act_table(ACT.Sigmoid)
            act.dma_start(rbias[:], router_b.rearrange("(a e) -> a e", a=1).broadcast_to([P, E])
                          ).then_inc(s_rbias, 16)

            def act_turn_x(b, kc):
                g, par = b.g + 1, (b.n + 1) % 2
                act.wait_ge(s_turnx, g * KC + kc + 1)
                if b.n >= 1:
                    act.wait_ge(s_z, (g - 1) * KC)
                    act.wait_ge(s_up, (g - 1) * NU)
                nc.scalar.activation(xq[:, par, kc, :], spare[:], ACT.Copy, scale=0.5).then_inc(s_xq, 1)
                nc.scalar.activation(xs[0][:, par, kc, :], spare[:], ACT.Copy, scale=0.5).then_inc(s_xhi, 1)

            def act_sigmoid(b):
                act.wait_ge(s_lg, b.g + 2)
                if b.n >= 0:
                    act.wait_ge(s_comb, b.g + 1)
                nc.scalar.activation(sg[:], lg[:], ACT.Sigmoid).then_inc(s_sg, 1)
                nc.scalar.preload_act_table(ACT.Gelu)

            def act_turn_g(b):
                act.wait_ge(s_turng, b.g + 2)
                if b.n >= 0:
                    act.wait_ge(s_gdram, (b.g + 1) * 16)
                nc.scalar.activation(combt[:], spare[0:E, :], ACT.Copy).then_inc(s_combt, 1)

            def act_out(b, part):
                g = b.g - 1 - part
                act.wait_ge(s_turno, g * 2 + part + 1)
                if b.n - 1 - part >= 1:
                    act.wait_ge(s_out[part], 16 * TT * g)
                nc.scalar.activation(o_tok[:, part].rearrange("p j c -> p (j c)"),
                                     spare[:], ACT.Copy).then_inc(s_otok, 1)

            def act_unit(b, u):
                kind, m = UNITS[u]
                act.wait_ge(s_up, b.g * NU + u + 1)
                if kind == EXPERT:
                    n = n_exp[u] - 1
                    if n >= NH:
                        act.wait_ge(s_prod, b.g * NU + n_exp.index(n - NH + 1) + 1)
                    elif b.n > 0:
                        act.wait_ge(s_prod, (b.g - 1) * NU + n_exp.index(NE + n - NH + 1) + 1)
                    nc.scalar.activation(act32[:, n % NH], up_ps[ring_at[u] % RING][:], ACT.Gelu,
                                         scale=1.0 / UP).then_inc(s_gelu, 1)
                else:
                    n = n_sha[u] - 1
                    if b.n > 0 or n >= 1:
                        act.wait_ge(s_su, b.g * NS + n)
                    nc.scalar.activation(half32[:], up_ps[ring_at[u] % RING][:], ACT.Tanh,
                                         scale=0.5 / UP).then_inc(s_tanh, 1)

            def act_high(b, back, u):
                g = b.g - back
                act.wait_ge(s_prod, g * NU + u + 1)
                if b.n - back > 0 or u >= NR:
                    act.wait_ge(s_down, g * NU + u - NR + 1)
                nc.scalar.activation(hid[0][:, u % NR], prod32[:, u % NH], ACT.Copy).then_inc(s_hi, 1)

            def act_z(b):
                act.wait_ge(s_z, b.g * KC)
                nc.scalar.activation(flat(zs[0][:]), flat(zq[:, (b.n - 1) % 2]), ACT.Copy
                                     ).then_inc(s_zhi, 1)

            def act_gate(b, s):
                r = b.g - 1
                act.wait_ge(s_step, r * TG + s + 1)
                nc.scalar.activation(th[:, s % 2].rearrange("p k b -> p (k b)"), gate_sums(s), ACT.Tanh,
                                     scale=0.5 / UP).then_inc(s_th, 1)

            def act_h(b, s):
                r = b.g - 1
                act.wait_ge(s_pre, r * TG + s + 1)
                if b.n > 1 and s in (0, HALF):
                    act.wait_ge(s_och, r * 2 if s else r * 2 - 1)
                src = flat3(pre[:, s % 2])
                nc.scalar.activation(flat3(hist[:, s]), src, ACT.Tanh).then_inc(s_h, 1)
                nc.scalar.activation(flat3(hs[0][:, s % 2]), src, ACT.Tanh).then_inc(s_hhi, 1)

            def spare_use(b, u):
                use = {TURN_X: act_turn_x, TURN_G: lambda b, _: act_turn_g(b), OUT: act_out, LOGITS: lambda b, _: None}
                for what, part, slot in SPARE:
                    if slot == u and b.there(what, part, b.n):
                        use[what](b, part)

            def body(b):
                for u in range(NU):
                    s = u - REC_SLOT
                    rec = b.tail and 0 <= s < TG
                    if rec:
                        act_gate(b, s)
                    if u > 0 and b.units:
                        act_high(b, 0, u - 1)
                    elif u == 0 and b.tail:
                        act_high(b, 1, NU - 1)
                    if rec:
                        act_h(b, s)
                    if b.units:
                        act_unit(b, u)
                    convs(b, u)
                    if b.n == 0 and u == SETUP_SLOT + 1:
                        recurrence_setup()
                    if u == 2 and b.tail:
                        act_z(b)
                    if u == SIGMOID_SLOT and b.prep:
                        act_sigmoid(b)
                    spare_use(b, u)

            def convs(b, u):
                for n in range(len(CONV)):
                    if b.n == 0 and CONV_SLOT[n] == u:
                        conv(n)

            def conv(n):
                _, dst, k, w = conv_parts(CONV[n])
                act.wait_ge(s_stage[n % NSTAGE], 16 * (n // NSTAGE + 1))
                nc.scalar.activation(dst[0], stage[:, n % NSTAGE, 0:k * w], ACT.Copy, scale=WUP
                                     ).then_inc(s_convhi, 1)

            act.wait_ge(s_condt, 1)
            prologue = Body(-1, -1)
            act_turn_x(prologue, 0)
            act_turn_x(prologue, 1)
            act_sigmoid(prologue)
            for n in range(len(CONV)):
                if CONV_SLOT[n] < 0:
                    conv(n)
                if n == 1:
                    act_turn_g(prologue)

            def recurrence_setup():
                for i in range(2):
                    act.wait_ge(s_turn0, i + 1)
                    nc.scalar.activation(flat3(gwt[0][:, KC * i:KC * i + KC]), gate_ps[i][:], ACT.Copy,
                                         scale=(UP, WUP)[i]).then_inc(s_gwhi, 1)
                nc.scalar.activation(hist[:, TG - 1], cond_t[:, :, 0, :], ACT.Copy).then_inc(s_h, 1)
                nc.scalar.activation(hs[0][:, 1], cond_t[:, :, 0, :], ACT.Copy).then_inc(s_hhi, 1)

            run_bodies(act, body)

        @block.vector
        def _(dve):
            done = [0]

            def link(ins):
                done[0] += 1
                ins.then_inc(s_const, 1)
                dve.wait_ge(s_const, done[0])

            def low_x(b, kc):
                g, par = b.g + 1, (b.n + 1) % 2
                dve.wait_ge(s_xhi, g * KC + kc + 1)
                dve.tensor_tensor(xs[1][:, par, kc, :], xq[:, par, kc, :], xs[0][:, par, kc, :],
                                  ALU.subtract).then_inc(s_xlo, 1)

            def logits(b):
                g = b.g + 1
                dve.wait_ge(s_lgps, g + 1)
                if b.n >= 0:
                    dve.wait_ge(s_sg, g)
                dve.scalar_tensor_tensor(lg[:], spare[:, 0:NJ * E].rearrange("p (j e) -> p j e", e=E), 1.0 / UP,
                                         every_tile(cond_lg), ALU.mult, ALU.add).then_inc(s_lg, 1)

            R_STEPS = 10

            def route(b, first, last):
                g = b.g + 1
                def step(n, *ins):
                    if first <= n <= last:
                        if n > 0:
                            dve.wait_ge(s_route, g * R_STEPS + n)
                        elif b.n >= 0:
                            dve.wait_ge(s_turng, g)
                        for i in ins:
                            last_i = i()
                        if n < R_STEPS:
                            last_i.then_inc(s_route, 1)
                        else:
                            last_i.then_inc(s_comb, 1)

                if first == 0:
                    dve.wait_ge(s_sg, g + 1)
                step(0, lambda: dve.tensor_tensor(sel[:, :, 0:E], sg[:], every_tile(rbias), ALU.add))
                step(1, lambda: dve.memset(fence[:], 0.0), *[(lambda j=j: dve.max(top8[:, j], sel[:, j, 0:E])) for j in range(NJ)])
                step(2, lambda: dve.tensor_copy(seek[:, :, 0:TOPK], top8[:, :, 0:TOPK]))
                step(3, lambda: dve.memset(fence[:], 0.0), *[(lambda j=j: dve.match_replace(left[:, j], seek[:, j], sel[:, j], TAKEN))
                          for j in range(NJ)])
                step(4, lambda: dve.tensor_tensor(mask[:], left[:, :, 0:E], sel[:, :, 0:E], ALU.not_equal))
                step(5, lambda: dve.tensor_tensor(smask[:], mask[:], sg[:], ALU.mult))
                step(6, lambda: dve.tensor_reduce(den[:], smask[:], AX_X, ALU.add))
                step(7, lambda: dve.tensor_scalar(deps[:], den[:], 1e-9, None, ALU.add),
                     lambda: dve.tensor_scalar(okay[:], den[:], 1e-9, None, ALU.is_gt))
                step(8, lambda: dve.reciprocal(drec[:], deps[:]),
                     lambda: dve.tensor_scalar(alt[:], okay[:], -1.0 / TOPK, 1.0 / TOPK, ALU.mult, ALU.add))
                step(9, lambda: dve.tensor_tensor(part_b[:], mask[:], bcast(alt), ALU.mult),
                     lambda: dve.tensor_tensor(okrec[:], drec[:], okay[:], ALU.mult))
                step(10, lambda: gates_end(g))

            def gates_end(g):
                dve.tensor_tensor(part_a[:], smask[:], bcast(okrec), ALU.mult).then_inc(s_gates, 1)
                dve.wait_ge(s_gates, g + 1)
                return dve.tensor_tensor(comb[:], part_a[:], part_b[:], ALU.add)

            def product(b, u):
                kind, m = UNITS[u]
                if b.n > 0 or u >= NH:
                    dve.wait_ge(s_lo, b.g * NU + u - NH + 1)
                    dve.wait_ge(s_hi, b.g * NU + u - NH + 1)
                if kind == EXPERT:
                    n = n_exp[u] - 1
                    dve.wait_ge(s_gelu, b.g * NE + n + 1)
                    if b.n == 0 and m == 0:
                        dve.wait_ge(s_spr_first, 16)
                    if m == (4 if b.n == 0 else 0):
                        dve.wait_ge(s_spr[b.n % 2], b.spreads * 16)
                    dve.tensor_tensor(prod32[:, u % NH], act32[:, n % NH], spread[:, b.n % 2, m // 2, :],
                                      ALU.mult).then_inc(s_prod, 1)
                else:
                    n = n_sha[u] - 1
                    r = ring_at[u]
                    dve.wait_ge(s_tanh, b.g * NS + n + 1)
                    dve.scalar_tensor_tensor(prod32[:, u % NH], half32[:], 1.0, up_ps[r % RING][:],
                                             ALU.add, ALU.mult).then_inc(s_su, 1)
                    dve.wait_ge(s_su, b.g * NS + n + 1)
                    dve.scalar_tensor_tensor(prod32[:, u % NH], prod32[:, u % NH], 0.5 / (UP * UP),
                                             up_ps[(r + 1) % RING][:], ALU.mult, ALU.mult).then_inc(s_prod, 1)

            def low(b, back, u):
                g = b.g - back
                dve.wait_ge(s_hi, g * NU + u + 1)
                if b.n - back > 0 or u >= NR:
                    dve.wait_ge(s_down, g * NU + u - NR + 1)
                dve.tensor_tensor(hid[1][:, u % NR], prod32[:, u % NH], hid[0][:, u % NR], ALU.subtract
                                  ).then_inc(s_lo, 1)

            def residual(b):
                par = (b.n - 1) % 2
                dve.wait_ge(s_down, b.g * NU)
                if b.n >= 3:
                    dve.wait_ge(s_och, (b.g - 3) * 2 + 2)
                for kc in range(KC):
                    dve.scalar_tensor_tensor(zq[:, par, :, kc, :],
                                             y_ps[kc][:].rearrange("p (t b) -> p t b", b=NB), MEAN,
                                             xq[:, par, kc, :].rearrange("p (t b) -> p t b", b=NB),
                                             ALU.mult, ALU.add).then_inc(s_z, 1)

            def low_z(b):
                dve.wait_ge(s_zhi, b.g)
                dve.tensor_tensor(flat(zs[1][:]), flat(zq[:, (b.n - 1) % 2]), flat(zs[0][:]), ALU.subtract
                                  ).then_inc(s_zlo, 1)

            def rec_pre(b, s):
                r = b.g - 1
                z = zq[:, (b.n - 1) % 2, s]
                dve.wait_ge(s_th, r * TG + s + 1)
                dve.scalar_tensor_tensor(flat3(gz[:]), flat3(th[:, s % 2]), 1.0, flat3(z), ALU.add, ALU.mult
                                         ).then_inc(s_gz, 1)
                dve.wait_ge(s_gz, r * TG + s + 1)
                dve.wait_ge(s_hl, r * TG + s + 1)
                dve.tensor_tensor(flat3(pre[:, s % 2]), flat3(gz[:]), flat3(hl[:, s % 2]), ALU.add
                                  ).then_inc(s_pre, 1)

            def rec_low(b, s):
                r = b.g - 1
                dve.wait_ge(s_hhi, r * TG + s + 2)
                dve.tensor_tensor(flat3(hs[1][:, s % 2]), flat3(hist[:, s]), flat3(hs[0][:, s % 2]),
                                  ALU.subtract).then_inc(s_hlo, 1)

            def out_channels(b, part):
                g = b.g - 1 - part
                par = (b.n - 1 - part) % 2
                if part == 1 or b.n > 1:
                    dve.wait_ge(s_turno, g * 2 + part)
                if part == 1:
                    dve.wait_ge(s_h, (g + 1) * TG + 1)
                else:
                    dve.wait_ge(s_h, g * TG + HALF + 1)
                for kc in range(KC):
                    ins = dve.scalar_tensor_tensor(o_ch[:, kc], zq[:, par, part * HALF:(part + 1) * HALF, kc, :],
                                                   2.0, hist[:, part * HALF:(part + 1) * HALF, kc, :],
                                                   ALU.mult, ALU.add)
                ins.then_inc(s_och, 1)

            def body(b):
                for u in range(NU):
                    s = u - REC_SLOT
                    rec = b.tail and 0 <= s < TG
                    if rec:
                        rec_pre(b, s)
                    if u > 0 and b.units:
                        low(b, 0, u - 1)
                    elif u == 0 and b.tail:
                        low(b, 1, NU - 1)
                    if rec:
                        rec_low(b, s)
                    if u == 2 and b.tail:
                        residual(b)
                    if u == 3 and b.tail:
                        low_z(b)
                    if b.units:
                        product(b, u)
                    convs(b, u)
                    if b.n == 0 and u == SETUP_SLOT - 1:
                        constants()
                    if b.n == 0 and u == SETUP_SLOT + 1:
                        recurrence_setup()
                    if u == 1 and b.late:
                        out_channels(b, 1)
                    if b.prep:
                        for what, part, slot in SPARE:
                            if what == TURN_X and slot == u:
                                low_x(b, part)
                        if u == SIGMOID_SLOT - 1:
                            logits(b)
                        if u == ROUTE_SLOT:
                            route(b, 0, 5)
                        if u == ROUTE_SLOT + 1:
                            route(b, 6, R_STEPS)
                    if u == REC_SLOT + HALF - 1 and b.tail:
                        out_channels(b, 0)

            def convs(b, u):
                for n in range(len(CONV)):
                    if b.n == 0 and CONV_SLOT[n] == u:
                        conv(n)

            def conv(n):
                _, dst, k, w = conv_parts(CONV[n])
                dve.wait_ge(s_convhi, n + 1)
                dve.scalar_tensor_tensor(dst[1], stage[:, n % NSTAGE, 0:k * w], WUP, dst[0],
                                         ALU.mult, ALU.subtract).then_inc(s_conv, 1)

            link(dve.memset(sel[:], PAD))
            link(dve.memset(seek[:], PAD))
            dve.wait_ge(s_clg_ps, 1)
            for t in range(TT):
                ins = dve.tensor_copy(cond_t[:, :, t, :], bank[0][:, 0:STEP].rearrange("p (k b) -> p k b", k=KC))
            ins.then_inc(s_condt, 1)
            dve.wait_ge(s_rw, 16)
            link(dve.tensor_scalar(rwx[0][:], rw[:, 0:KC, :], WUP, None, ALU.mult))
            link(dve.scalar_tensor_tensor(rwx[1][:], rw[:, 0:KC, :], WUP, rwx[0][:], ALU.mult, ALU.subtract))
            assert done[0] == N_ROUTER_CONST
            prologue = Body(-1, -1)
            low_x(prologue, 0)
            low_x(prologue, 1)
            dve.wait_ge(s_clg_ps, 2)
            link(dve.tensor_copy(cond_lg[:], bank[1][:, 0:E]))
            logits(prologue)
            dve.wait_ge(s_rbias, 16)
            route(prologue, 0, R_STEPS)
            for n in range(len(CONV)):
                if CONV_SLOT[n] < 0:
                    conv(n)
            def constants():
                dve.wait_ge(s_small, 16 * SMALL)
                link(dve.memset(ones[:], 1.0))
                link(dve.memset(ones2[:], 1.0))
                dve.wait_ge(s_ident, 2)
                link(dve.tensor_scalar(al1[:], al[:], -1.0, 1.0, ALU.mult, ALU.add))
                for kc in range(KC):
                    link(dve.tensor_scalar(leak[:, kc, :], ones[:, 0:NB], al1[:, kc:kc + 1], None, ALU.mult))
                link(dve.tensor_scalar(gb_full[:], gb_in[:], UP, None, ALU.mult))
                link(dve.tensor_copy(gb_hi[:], gb_full[:]))
                link(dve.tensor_tensor(gb_lo[:], gb_full[:], gb_hi[:], ALU.subtract))
                link(dve.tensor_scalar(gb_lo2[:], gb_lo[:], ident[0:2, 1:2], None, ALU.mult))
                link(dve.scalar_tensor_tensor(gb[:], gb_hi[:], ident[0:2, 0:1], gb_lo2[:], ALU.mult, ALU.add))
                assert done[0] == N_CONST

            def recurrence_setup():
                for i in range(2):
                    dve.wait_ge(s_gwhi, i + 1)
                    dve.scalar_tensor_tensor(flat3(gwt[1][:, KC * i:KC * i + KC]), gate_ps[i][:], (UP, WUP)[i],
                                             flat3(gwt[0][:, KC * i:KC * i + KC]), ALU.mult, ALU.subtract
                                             ).then_inc(s_gwlo, 1)
                dve.wait_ge(s_hhi, 1)
                dve.tensor_tensor(flat3(hs[1][:, 1]), flat3(hist[:, TG - 1]), flat3(hs[0][:, 1]),
                                  ALU.subtract).then_inc(s_hlo, 1)

            run_bodies(dve, body)

        @block.tensor
        def _(pe):
            def pairs(out_ap, w, mov, start, stop, chunks):
                last, n = None, len(chunks) * 3
                for i, k in enumerate(chunks):
                    for j, (a, c) in enumerate(((0, 0), (1, 0), (0, 1))):
                        last = pe.matmul(out_ap, w(a, k), mov(c, k), start=start and i == 0 and j == 0,
                                         stop=stop and i * 3 + j == n - 1, skip_group_check=True)
                return last

            def up(b, u):
                kind, m = UNITS[u]
                par = b.n % 2
                r = ring_at[u]

                def free(slot):
                    before = slot - RING
                    back = 0
                    if before < 0:
                        before, back = before + at, 1
                    if b.n - back < 0:
                        return
                    v = max(i for i in range(NU) if ring_at[i] <= before)
                    if UNITS[v][0] == EXPERT:
                        pe.wait_ge(s_gelu, (b.g - back) * NE + n_exp[v])
                    elif before == ring_at[v] + 1:
                        pe.wait_ge(s_prod, (b.g - back) * NU + v + 1)
                    else:
                        pe.wait_ge(s_su, (b.g - back) * NS + n_sha[v])

                mov = lambda c, k: xs[c][:, par, k, :]
                if u == 0:
                    pe.wait_ge(s_xlo, b.g * KC + KC)
                if kind == EXPERT:
                    e, h = m // 2, m % 2
                    conv_ready(pe, b.n, ("w1e", e))
                    free(r)
                    pairs(up_ps[r % RING][:], lambda a, k: w1e_s[a][:, e, k, h * P:(h + 1) * P], mov,
                          True, True, range(KC)).then_inc(s_up, 1)
                else:
                    for i in range(2):
                        conv_ready(pe, b.n, ("w13", i))
                        free(r + i)
                        last = pairs(up_ps[(r + i) % RING][:], lambda a, k: w13_s[a][:, i, k, m * P:(m + 1) * P],
                                     mov, True, True, range(KC))
                    last.then_inc(s_up, 1)

            def down(b, back, u):
                kind, m = UNITS[u]
                g = b.g - back
                e, h = m // 2, m % 2
                conv_ready(pe, b.n - back, ("w2e", e) if kind == EXPERT else ("w2", 0))
                if u == 0 and b.n - back > 0:
                    pe.wait_ge(s_z, g * KC)
                pe.wait_ge(s_lo, g * NU + u + 1)
                for kc in range(KC):
                    cols = slice(kc * P, (kc + 1) * P)
                    last = pairs(y_ps[kc][:],
                                 lambda a, k: (w2e_s[a][:, e, h, cols] if kind == EXPERT else w2_s[a][:, m, cols]),
                                 lambda c, k: hid[c][:, u % NR], u == 0, u == NU - 1, [0])
                last.then_inc(s_down, 1)

            def gate_fill(b):
                if b.n == 1:
                    pe.wait_ge(s_gwlo, 2)
                    pe.wait_ge(s_const, N_CONST)
                pe.wait_ge(s_zlo, b.g)
                for hf in range(2):
                    if b.n > 1:
                        pe.wait_ge(s_th, (b.g - 1) * TG if hf else (b.g - 1) * TG - HALF)
                    for jc in range(KC):
                        cols = slice(jc * P, (jc + 1) * P)
                        dst = gate_ps[hf][:].rearrange("p (t k b) -> p t k b", k=KC, b=NB)[:, :, jc, :]
                        pe.matmul(dst, gb[:, cols], ones2[:].rearrange("p (t b) -> p t b", b=NB),
                                  start=jc == 0, stop=False, skip_group_check=True)
                        pairs(dst, lambda a, k: gwt[a][:, KC + k, cols],
                              lambda c, k: zs[c][:, hf * HALF:(hf + 1) * HALF, k, :], False, False, range(KC))

            def gate_step(b, s):
                r = b.g - 1
                for c, weights, ready in ((0, (0, 1), s_hhi), (1, (0,), s_hlo)):
                    pe.wait_ge(ready, r * TG + s + 1)
                    for jc in range(KC):
                        for a in weights:
                            for k in range(KC):
                                last = pe.matmul(gate_sums(s)[:, jc * NB:(jc + 1) * NB], gwt[a][:, k, jc * P:(jc + 1) * P],
                                                 hs[c][:, (s - 1) % 2, k, :], start=False, stop=False,
                                                 skip_group_check=True)
                last.then_inc(s_step, 1)

            def spare_use(b, pos):
                what, part, _ = SPARE[pos]
                if not b.there(what, part, b.n):
                    return
                ps = spare
                released(pe, b, pos)
                if what == TURN_X:
                    g, par = b.g + 1, (b.n + 1) % 2
                    if part == 0:
                        pe.wait_ge(s_x[par], b.loads * (16 * TT))
                    for j in range(NJ):
                        last = pe.transpose(ps[:, j * P:(j + 1) * P], x_tok[:, par, j, part * P:(part + 1) * P],
                                            ident[:])
                    last.then_inc(s_turnx, 1)
                elif what == LOGITS:
                    g, par = b.g + 1, (b.n + 1) % 2
                    pe.wait_ge(s_xlo, g * KC + KC)
                    for j in range(NJ):
                        last = pairs(ps[:, j * E:(j + 1) * E],
                                     lambda a, k: xs[a][:, par, k, j * P:(j + 1) * P],
                                     lambda c, k: rwx[c][:, k, :], True, True, range(KC))
                    last.then_inc(s_lgps, 1)
                elif what == TURN_G:
                    pe.wait_ge(s_comb, b.g + 2)
                    for j in range(NJ):
                        last = pe.transpose(ps[0:E, j * P:(j + 1) * P], comb[:, j, :], ident[:])
                    last.then_inc(s_turng, 1)
                else:
                    g = b.g - 1 - part
                    pe.wait_ge(s_och, g * 2 + part + 1)
                    for j in range(NJ // 2):
                        for kc in range(KC):
                            last = pe.transpose(ps[:, j * C + kc * P:j * C + (kc + 1) * P],
                                                o_ch[:, kc, j * TT:(j + 1) * TT, :].rearrange("p t b -> p (t b)"),
                                                ident[:])
                    last.then_inc(s_turno, 1)

            def body(b):
                for u in range(NU):
                    if b.units:
                        up(b, u)
                    if u == REC_SLOT and b.tail:
                        gate_fill(b)
                    s = u - REC_SLOT
                    if b.tail and 0 <= s < TG:
                        gate_step(b, s)
                    if u < DOWN_LAG:
                        if b.tail:
                            down(b, 1, NU - DOWN_LAG + u)
                    elif b.units:
                        down(b, 0, u - DOWN_LAG)
                    for pos, (what, part, slot) in enumerate(SPARE):
                        if slot == u:
                            spare_use(b, pos)
                    if b.n == 0 and u == SETUP_SLOT:
                        recurrence_setup()

            pe.wait_ge(s_ident, 2)
            pe.wait_ge(s_cond, 16)
            for k in range(KC):
                last = pe.transpose(bank[0][:, k * NB:(k + 1) * NB], cond_in[:, k * P:(k + 1) * P],
                                    ident[0:NB, 0:NB])
            last.then_inc(s_clg_ps, 1)
            prologue = Body(-1, -1)
            PROLOGUE = [p for p, u in enumerate(SPARE) if u[0] != OUT]
            spare_use(prologue, PROLOGUE[0])
            spare_use(prologue, PROLOGUE[1])
            pe.wait_ge(s_condt, 1)
            pe.wait_ge(s_rw, 16)
            for k in range(KC):
                last = pe.matmul(bank[1][:, 0:E], cond_t[:, k].rearrange("p t b -> p (t b)"), rw[:, KC + k, :],
                                 start=k == 0, stop=k == KC - 1)
            last.then_inc(s_clg_ps, 1)
            pe.wait_ge(s_const, N_ROUTER_CONST)
            for p in PROLOGUE[2:]:
                spare_use(prologue, p)

            def recurrence_setup():
                pe.wait_ge(s_gw, 16)
                for i in range(2):
                    for k in range(KC):
                        for jc in range(KC):
                            c0 = (i * KC + k) * P
                            last = pe.transpose(gate_ps[i][:, k * C + jc * P:k * C + (jc + 1) * P],
                                                gw[:, jc, c0:c0 + P], ident[:])
                    last.then_inc(s_turn0, 1)

            run_bodies(pe, body)


_INS = ['x', 'cond_1024', 'L0_cond_router_W', 'L0_cond_router_bias', 'L0_cond_w1', 'L0_cond_w3', 'L0_cond_w2',
        'L0_cond_W1e', 'L0_cond_W2e', 'L1_cond_W', 'L1_cond_b', 'L1_cond_alpha']
_OUTS = [((32, 256, 256), 'float32')]


def kernel(**inputs):
    import numpy as _np
    import concourse.bacc as _bacc
    from concourse import mybir as _mybir
    from concourse.bass_utils import run_bass_kernel_spmd as _run

    nc = _bacc.Bacc("TRN2", target_bir_lowering=False, num_devices=1)
    arrays, args = {}, []
    for name in _INS:
        a = _np.ascontiguousarray(inputs[name])
        arrays[f"in_{name}_dram"] = a
        args.append(nc.dram_tensor(f"in_{name}_dram", a.shape, _mybir.dt.from_np(a.dtype), kind="ExternalInput").ap())
    for i, (shape, dtype) in enumerate(_OUTS):
        dt = _mybir.dt.from_np(_np.dtype(dtype))
        args.append(nc.dram_tensor(f"out_{i}_dram", shape, dt, kind="ExternalOutput").ap())
    moe_gated_recurrence(nc, *args)
    r = _run(nc, [arrays], core_ids=[0])
    got = tuple(r.results[0][f"out_{i}_dram"] for i in range(len(_OUTS)))
    return got[0]
```

```python
from contextlib import ExitStack

import concourse.bass as bass
from concourse import mybir

F32 = mybir.dt.float32
F16 = mybir.dt.float16
I32 = mybir.dt.int32
ALU = mybir.AluOpType
ACT = mybir.ActivationFunctionType
AX_X = mybir.AxisListType.X

P = 128
TOPK = 2
N_SHARED = 1

EXPERT, SHARED = "expert", "shared"
NPAIR = 12
UNITS = [(EXPERT, p) for p in range(NPAIR)] + [(SHARED, m) for m in range(8)]
NU = len(UNITS)
NSH = NU - NPAIR
DOWN_LAG = 2

STEP_AT = {}
for _u in range(NU):
    for _half in (0, 1):
        if (_u, _half) not in ((0, 1), (2, 1), (4, 1), (5, 1), (7, 1), (8, 1), (10, 1), (11, 1)):
            STEP_AT[(_u, _half)] = len(STEP_AT)

TOKENS, TURN_X, OUT, LOGITS, RANKS, FIRST = "tokens", "turn_x", "out", "logits", "ranks", "first"
MISC = {2: (TURN_X, 0), 3: (TURN_X, 1), 4: (TURN_X, 2), 5: (TURN_X, 3), 6: (LOGITS, 0), 7: (OUT, 3), 8: (OUT, 0),
        9: (RANKS, 0), 12: (OUT, 1), 18: (OUT, 2)}
OWN_TURN = 5
SPARE = []
for _u in range(NU):
    if _u + 1 < OWN_TURN:
        SPARE.append((TOKENS, _u + 1, _u))
    if _u in MISC:
        SPARE.append(MISC[_u] + (_u,))
SPARE.append((FIRST, 0, NU - 1))

TAKEN = 3.0e38
PAD = -3.0e38
FAR = 8192.0
N_ROUTER_CONST = 8
N_CONST = 17
N_ROUTE_LINKS = 11
MASK_LINK = 5
N_PLACE_LINKS = 11
SLOT_LINK = 10


def moe_gated_recurrence(nc, x, cond, router_w, router_b, w1, w3, w2, w1e, w2e, gate_w, gate_b, alpha, out):
    NB, T, C = x.shape
    E, _, HE = w1e.shape
    HS = w1.shape[1]
    KC = C // P
    TT = P // NB
    NJ = 8
    TS = NJ * TT
    TG = TS // 2
    G = TG * NB
    NS = T // TS
    HALF = TG // 2
    STEP = KC * NB
    MID = HS // P
    NT = 2 * NPAIR
    assert KC == 2 and HE == 2 * P and MID == 4 and E == 8 and NS == 8 and len(STEP_AT) == TS
    assert (NJ * P * TOPK + E * (P - 1)) // P <= NT

    WUP = 64.0
    UP = 0.5 * WUP
    WDN = 64.0
    MEAN = 0.5 / ((N_SHARED + TOPK) * WDN)

    x_slots = [nc.dram_tensor(f"x_slots_{n}", [NT * P, C], F32).ap() for n in ("even", "odd")]
    y_slots = [nc.dram_tensor(f"y_slots_{n}", [NT * P, C], F32).ap() for n in ("even", "odd")]
    x_in = x.rearrange("b (g j t) c -> g t b j c", j=NJ, t=TT)
    out_v = out.rearrange("b (g q j t) c -> g q t b j c", q=4, j=2, t=TT)

    with ExitStack() as ctx:
        def sb(name, shape, dt=F32):
            return ctx.enter_context(nc.sbuf_tensor(name, shape, dt))

        def sem(name):
            return ctx.enter_context(nc.semaphore(name))

        bank = [ctx.enter_context(nc.psum_tensor(f"bank{i}", [P, 512], F32)) for i in range(8)]
        RING = 3
        ring = bank[0:RING]
        y_ps = bank[3:5]
        gate_ps = bank[5:7]
        spare = bank[7]

        HL = ("high", "low")
        w1e_s = [sb(f"w1e_{h}", [P, E, KC, HE], F16) for h in HL]
        w2e_s = [sb(f"w2e_{h}", [P, E, KC, C], F16) for h in HL]
        w13_s = [sb(f"w13_{h}", [P, 2, KC, HS], F16) for h in HL]
        w2_s = [sb(f"w2_{h}", [P, MID, C], F16) for h in HL]
        gw = sb("gw", [P, KC, 2 * C])
        gwt = [sb(f"gwt_{h}", [P, 2 * KC, C], F16) for h in HL]
        rw = sb("rw", [P, 2 * KC, E])
        rwx = [sb(f"rwx_{h}", [P, KC, E], F16) for h in HL]
        gb_in = sb("gb_in", [2, C])
        gb_full = sb("gb_full", [2, C])
        gb_hi = sb("gb_hi", [2, C], F16)
        gb_lo = sb("gb_lo", [2, C], F16)
        gb_lo2 = sb("gb_lo2", [2, C], F16)
        gb = sb("gb", [2, C], F16)
        ones2 = sb("ones2", [2, HALF * NB], F16)
        al = sb("al", [P, KC])
        leak = sb("leak", [P, KC])
        ident = sb("ident", [P, P])
        below = sb("below", [P, P], F16)
        ones16 = sb("ones16", [P, P], F16)
        cond_in = sb("cond_in", [NB, C])
        cond_t = sb("cond_t", [P, KC, TT, NB])
        cond_lg = sb("cond_lg", [P, E])
        rbias = sb("rbias", [P, E])
        zeros = sb("zeros", [P, 2 * C])

        x_tok = sb("x_tok", [P, 2, NJ, C])
        xq = sb("xq", [P, 2, KC, 2 * G])
        xs = [sb(f"xs_{h}", [P, 2, KC, 2 * G], F16) for h in HL]
        lg = sb("lg", [P, NJ, E])
        sg = sb("sg", [P, NJ, E])
        sel = sb("sel", [P, NJ, 16])
        top8 = sb("top8", [P, NJ, 8])
        seek = sb("seek", [P, NJ, 8])
        left = sb("left", [P, NJ, 16])
        fence = sb("fence", [P, 1])
        fence_pool = sb("fence_pool", [P, 1])
        mask = sb("mask", [P, NJ, E])
        mask16 = sb("mask16", [P, NJ, E], F16)
        smask = sb("smask", [P, NJ, E])
        den = sb("den", [P, NJ])
        deps = sb("deps", [P, NJ])
        drec = sb("drec", [P, NJ])
        okay = sb("okay", [P, NJ])
        okrec = sb("okrec", [P, NJ])
        alt = sb("alt", [P, NJ])
        part_a = sb("part_a", [P, NJ, E])
        part_b = sb("part_b", [P, NJ, E])
        comb = sb("comb", [P, NJ, E])
        full_at = sb("full_at", [P, 8])
        tile_no = sb("tile_no", [P, NT])
        ranks = sb("ranks", [P, NJ * E + E])
        opened = sb("opened", [P, E, 8])
        scan = [sb(f"scan{i}", [P, 2 * E]) for i in range(3)]
        tile_end = sb("tile_end", [P, E])
        tile_base = sb("tile_base", [P, E])
        past = sb("past", [P, NT, E])
        owner_f = sb("owner_f", [P, NT])
        owner_c = sb("owner_c", [P, NT])
        owner = sb("owner", [P, 2, NPAIR], I32)
        slot = sb("slot", [P, NJ, E])
        slot_up = sb("slot_up", [P, NJ, E])
        slot_dn = sb("slot_dn", [P, NJ, E])
        top_slot = sb("top_slot", [P, NJ])
        low_slot = sb("low_slot", [P, NJ])
        is_top = sb("is_top", [P, NJ, E])
        is_low = sb("is_low", [P, NJ, E])
        gate_top = sb("gate_top", [P, NJ, E])
        gate_low = sb("gate_low", [P, NJ, E])
        where = sb("where", [P, 2, NJ, TOPK], I32)
        gate2 = sb("gate2", [P, 2, NJ, TOPK])
        NIN = 3
        x_pair = sb("x_pair", [P, NIN, 2, C])
        xe = [sb(f"xe_{h}", [P, 2, KC, 2 * P], F16) for h in HL]
        act32 = sb("act32", [P, 2, 512])
        NR = 4
        hid = [sb(f"hid_{h}", [P, NR, 512], F16) for h in HL]
        NYS = 3
        y_pair = sb("y_pair", [P, NYS, 2 * C])
        NYG = 4
        y_got = sb("y_got", [P, NYG, TOPK, C])
        r_part = sb("r_part", [P, 2, C])
        r_sum = sb("r_sum", [P, NYG, C])
        half32 = sb("half32", [P, G])
        prod32 = sb("prod32", [P, 2, G])
        zq = sb("zq", [P, 2, TS, KC, NB])
        zr = sb("zr", [P, 2, KC, NB, 2])
        zs = [sb(f"zs_{h}", [P, 2, TG, KC, NB], F16) for h in HL]
        hist = sb("hist", [P, TS, KC, NB])
        hs = [sb(f"hs_{h}", [P, 2, KC, NB], F16) for h in HL]
        th = sb("th", [P, 2, KC, NB, 2])
        pre = sb("pre", [P, 2, KC, NB, 2])
        o_ch = sb("o_ch", [P, KC, HALF, NB])
        o_tok = sb("o_tok", [P, 2, 2, C])

        NSTAGE = 4
        stage = zq[:].rearrange("p a t k b -> p (a t k b)").rearrange("p (n w) -> p n w", n=NSTAGE)

        s_x = [sem("s_x_even"), sem("s_x_odd")]
        s_rw = sem("s_rw")
        s_rbias = sem("s_rbias")
        s_small = sem("s_small")
        s_cond = sem("s_cond")
        s_gw = sem("s_gw")
        s_stage = [sem(f"s_stage{i}") for i in range(NSTAGE)]
        s_ident = sem("s_ident")
        s_zero0 = sem("s_zero0")
        s_zero = [sem("s_zero_even"), sem("s_zero_odd")]
        s_const = sem("s_const")
        s_convhi = sem("s_convhi")
        s_conv = sem("s_conv")
        s_turn0 = sem("s_turn0")
        s_gwhi = sem("s_gwhi")
        s_gwlo = sem("s_gwlo")
        s_condt = sem("s_condt")
        s_clg_ps = sem("s_clg_ps")
        s_xin = [sem(f"s_xin{i}") for i in range(NIN)]
        s_xt = sem("s_xt")
        s_xehi = sem("s_xehi")
        s_xelo = sem("s_xelo")
        s_up = sem("s_up")
        s_tanh = sem("s_tanh")
        s_su = sem("s_su")
        s_prod = sem("s_prod")
        s_hi = sem("s_hi")
        s_lo = sem("s_lo")
        s_down = sem("s_down")
        s_ev = sem("s_ev")
        s_yw = [sem(f"s_yw{i}") for i in range(NYS)]
        s_got = [sem(f"s_got{i}") for i in range(NYG)]
        s_rp = sem("s_rp")
        s_r = sem("s_r")
        s_y = sem("s_y")
        s_z = sem("s_z")
        s_zhi = sem("s_zhi")
        s_zlo = sem("s_zlo")
        s_step = sem("s_step")
        s_th = sem("s_th")
        s_rest = sem("s_rest")
        s_pre = sem("s_pre")
        s_h = sem("s_h")
        s_hhi = sem("s_hhi")
        s_hlo = sem("s_hlo")
        s_turnx = sem("s_turnx")
        s_xhi = sem("s_xhi")
        s_xlo = sem("s_xlo")
        s_lgps = sem("s_lgps")
        s_lg = sem("s_lg")
        s_sg = sem("s_sg")
        s_route = sem("s_route")
        s_comb = sem("s_comb")
        s_rkps = sem("s_rkps")
        s_rk = sem("s_rk")
        s_chain = sem("s_chain")
        s_placed = sem("s_placed")
        s_scat = sem("s_scat")
        s_fence = sem("s_fence")
        s_och = sem("s_och")
        s_turno = sem("s_turno")
        s_otok = sem("s_otok")
        s_out = [sem(f"s_out{i}") for i in range(4)]

        class Body:
            def __init__(self, g, n, half=None):
                self.g, self.n = g, n
                self.half = n // 2 if half is None else half
                self.units = 0 <= n < NS
                self.tail = 1 <= n <= NS
                self.prep = n + 1 < NS
                self.late = 2 <= n <= NS + 1

            def there(self, what, part, n):
                if what == OUT:
                    return (1 <= n <= NS) if part < 3 else (2 <= n <= NS + 1)
                if what == TOKENS:
                    return 0 <= n < NS
                return 0 <= n + 1 < NS

        def released(eng, body, pos):
            p, back = pos, 0
            while True:
                p -= 1
                if p < 0:
                    p, back = len(SPARE) - 1, back + 1
                if body.n - back < -1:
                    return
                if body.there(*SPARE[p][0:2], body.n - back):
                    break
            what, part, _ = SPARE[p]
            g = body.g - back
            if what == TOKENS:
                eng.wait_ge(s_xelo, g * NPAIR + part + 1)
            elif what == FIRST:
                eng.wait_ge(s_xelo, g * NPAIR + NPAIR + 1)
            elif what == TURN_X:
                eng.wait_ge(s_xhi, g * 4 + 4 + part + 1)
            elif what == OUT:
                eng.wait_ge(s_otok, g * 4 - (8 if part == 3 else 4) + part + 1)
            elif what == LOGITS:
                eng.wait_ge(s_lg, g + 2)
            else:
                eng.wait_ge(s_rk, g + 2)

        USES = []
        for u, (kind, _) in enumerate(UNITS):
            USES += [("up", u)] if kind == EXPERT else [("first", u), ("second", u)]
            if DOWN_LAG <= u < NPAIR + DOWN_LAG:
                USES.append(("down", u - DOWN_LAG))
        USES_TO = -(-len(USES) // RING) * RING
        n_sha = [sum(k == SHARED for k, _ in UNITS[:u + 1]) for u in range(NU)]

        def loads(b):
            return b.half + (1 if b.n % 2 == 0 else 2)

        def turn_bank(b, i):
            return spare if b.n >= 0 else (y_ps[0], y_ps[1], gate_ps[0], spare)[i]

        def pair_bank(p):
            return y_ps[p % 2] if p >= OWN_TURN else spare

        def ring_bank(what, u):
            return ring[USES.index((what, u)) % RING]

        def ring_free(eng, b, what, u):
            at, back = USES.index((what, u)) - RING, 0
            if at < 0:
                at, back = at + USES_TO, 1
                while at >= len(USES):
                    at -= RING
            if b.n - back < 0:
                return
            what, u = USES[at]
            g = b.g - back
            if what == "up":
                eng.wait_ge(s_hi, g * NU + u + 1)
            elif what == "first":
                eng.wait_ge(s_su, g * NSH + n_sha[u])
            elif what == "second":
                eng.wait_ge(s_prod, g * NSH + n_sha[u])
            else:
                eng.wait_ge(s_ev, g * NPAIR + u + 1)

        CONV = [("w1e", i) for i in range(0, E, 2)] + [("w2e", i) for i in range(0, E, 2)]
        N_EXPERT_CONV = len(CONV)
        CONV += [("w13", 0), ("w13", 1), ("w2", 0)]
        CONV_SLOT = [-1] * N_EXPERT_CONV + [5, 7, 9]

        def conv_parts(key):
            kind, i = key
            if kind in ("w1e", "w2e"):
                src = (w1e if kind == "w1e" else w2e)[i:i + 2].rearrange("e (k p) h -> p e k h", p=P)
                dst = [w[:, i:i + 2] for w in (w1e_s if kind == "w1e" else w2e_s)]
                return src, [d.rearrange("p e k h -> p (e k h)") for d in dst], 2, 2, 256
            if kind == "w13":
                src, dst = (w1, w3)[i].rearrange("(k p) h -> p k h", p=P), [w[:, i] for w in w13_s]
                return src, [d.rearrange("p k h -> p (k h)") for d in dst], 1, KC, HS
            src, dst = w2.rearrange("(k p) h -> p k h", p=P), [w[:, :, :] for w in w2_s]
            return src, [d.rearrange("p k h -> p (k h)") for d in dst], 1, MID, C

        def run_bodies(eng, body):
            for n in range(2):
                body(Body(n, n))
            with eng.Fori(1, NS // 2 - 1) as i:
                body(Body(i * 2, 2, i))
                body(Body(i * 2 + 1, 3, i))
            for n in range(NS - 2, NS + 2):
                body(Body(n, n))

        def bcast(ap):
            return ap[:].rearrange("p (j a) -> p j a", a=1).broadcast_to([P, NJ, E])

        def every_tile(ap):
            return ap[:].rearrange("p (a e) -> p a e", a=1).broadcast_to([P, NJ, E])

        def flat(ap):
            return ap.rearrange("p t k b -> p (t k b)")

        def flat3(ap):
            return ap.rearrange("p k b -> p (k b)")

        def gate_sums(s):
            at_col = (s % HALF) * STEP
            return gate_ps[(s // HALF) % 2][:, at_col:at_col + STEP]

        block = ctx.enter_context(nc.Block())

        @block.sync
        def _(sp):
            def load_x(g, par):
                for t in range(TT):
                    sp.dma_start(x_tok[NB * t:NB * (t + 1), par, :, :], x_in[g, t]).then_inc(s_x[par], 16)

            def load_weight(n):
                src, _, a, k, w = conv_parts(CONV[n])
                if n >= NSTAGE:
                    sp.wait_ge(s_conv, n - NSTAGE + 1)
                dst = stage[:, n % NSTAGE, 0:a * k * w]
                if a == 1:
                    sp.dma_start(dst.rearrange("p (k w) -> p k w", k=k), src).then_inc(s_stage[n % NSTAGE], 16)
                else:
                    sp.dma_start(dst.rearrange("p (a k w) -> p a k w", a=a, k=k), src
                                 ).then_inc(s_stage[n % NSTAGE], 16)

            def load_pair(par, p):
                sp.dma_start(x_pair[:, p % NIN], x_slots[par][2 * p * P:(2 * p + 2) * P, :].rearrange(
                    "(i p) c -> p i c", p=P)).then_inc(s_xin[p % NIN], 16)

            def next_section(b):
                sp.wait_ge(s_scat, (b.g + 2) * (16 * TOPK * NJ))
                for p in range(NIN):
                    if b.n >= 0:
                        sp.wait_ge(s_xt, b.g * NPAIR + NPAIR - NIN + p + 1)
                    load_pair((b.n + 1) % 2, p)

            def store(g, part):
                sp.wait_ge(s_otok, g * 4 + part + 1)
                for t in range(TT):
                    sp.dma_start(out_v[g, part, t], o_tok[NB * t:NB * (t + 1), part % 2, :, :]
                                 ).then_inc(s_out[part], 16)

            def body(b):
                for u in range(NU):
                    if u == 4 and 0 <= b.n and b.n + 2 < NS:
                        load_x(b.g + 2, b.n % 2)
                    if b.units and u + NIN < NPAIR:
                        sp.wait_ge(s_xt, b.g * NPAIR + u + 1)
                        load_pair(b.n % 2, u + NIN)
                    if b.units and 0 <= u - DOWN_LAG < NPAIR:
                        p = u - DOWN_LAG
                        sp.wait_ge(s_ev, b.g * NPAIR + p + 1)
                        sp.dma_start(y_slots[b.n % 2][2 * p * P:(2 * p + 2) * P, :].rearrange("(i p) c -> p i c", p=P),
                                     y_pair[:, p % NYS].rearrange("p (i c) -> p i c", i=2)).then_inc(s_yw[p % NYS], 16)
                    if MISC.get(u, (None,))[0] == OUT and b.there(*MISC[u], b.n):
                        part = MISC[u][1]
                        store(b.g - (2 if part == 3 else 1), part)
                if b.prep:
                    next_section(b)

            load_x(0, 0)
            for n in range(len(CONV)):
                if n == NSTAGE:
                    for k in range(KC):
                        sp.dma_start(al[:, k:k + 1], alpha.rearrange("(k p a) -> k p a", p=P, a=1)[k]
                                     ).then_inc(s_small, 16)
                    sp.dma_start(gb_in[:], gate_b.rearrange("(a c) -> a c", a=1).broadcast_to([2, C])
                                 ).then_inc(s_small, 16)
                    sp.dma_start(gw[:], gate_w.rearrange("(k p) c -> p k c", p=P)).then_inc(s_gw, 16)
                if n == N_EXPERT_CONV - 2:
                    load_x(1, 1)
                if n == N_EXPERT_CONV:
                    next_section(Body(-1, -1))
                load_weight(n)
            run_bodies(sp, body)
            for part in range(4):
                sp.wait_ge(s_out[part], 16 * TT * NS)

        @block.gpsimd
        def _(pool):
            nc.gpsimd.memset(zeros[:], 0.0).then_inc(s_zero0, 1)
            nc.gpsimd.memset(ident[:], 0.0).then_inc(s_ident, 1)
            nc.gpsimd.memset(below[:], 1.0).then_inc(s_ident, 1)
            pool.wait_ge(s_ident, 2)
            nc.gpsimd.affine_select(out=ident[:], in_=ident[:], compare_op=ALU.not_equal, fill=1.0,
                                    base=0, pattern=[[-1, P]], channel_multiplier=1).then_inc(s_ident, 1)
            nc.gpsimd.affine_select(out=below[:], in_=below[:], compare_op=ALU.is_gt, fill=0.0,
                                    base=0, pattern=[[1, P]], channel_multiplier=-1).then_inc(s_ident, 1)
            pool.iota(full_at[:], pattern=[[P, 8]], base=0, channel_multiplier=0,
                      allow_small_or_imprecise_dtypes=True).then_inc(s_ident, 1)
            pool.iota(tile_no[:], pattern=[[1, NT]], base=0, channel_multiplier=0,
                      allow_small_or_imprecise_dtypes=True).then_inc(s_ident, 1)

            def clear_slots(par):
                pool.dma_start(x_slots[par].rearrange("(a p i) c -> p a (i c)", p=P, i=2),
                               zeros[:].rearrange("p (a c) -> p a c", a=1).broadcast_to([P, NPAIR, 2 * C])
                               ).then_inc(s_zero[par], 16)

            pool.wait_ge(s_x[0], 16 * TT)
            pool.wait_ge(s_zero0, 1)
            clear_slots(0)

            FENCES = 6
            SCAT_FIRST = 5

            def pass_fence(count):
                pool.wait_ge(s_fence, count)
                nc.gpsimd.tensor_tensor(fence_pool[:], zeros[:, 0:1], zeros[:, 1:2], ALU.mult).then_inc(s_fence, 1)

            def at_slots(dram, par, j, k):
                return bass.IndirectOffsetOnAxis(ap=where[:, par, j, k:k + 1], axis=0)

            def scatter(b):
                par = (b.n + 1) % 2
                pool.wait_ge(s_x[par], loads(b) * (16 * TT))
                pool.wait_ge(s_chain, (b.g + 1) * N_PLACE_LINKS + SLOT_LINK)
                if b.n == 0:
                    pool.wait_ge(s_zero[1], 16)
                pass_fence(b.g * FENCES + 1)
                scatter_tiles(par, range(0, SCAT_FIRST))

            def scatter_tiles(par, tiles):
                for j in tiles:
                    for k in range(TOPK):
                        pool.indirect_dma_start(x_slots[par], at_slots(x_slots, par, j, k), x_tok[:, par, j, :], None
                                                ).then_inc(s_scat, 16)

            def gather(b, j):
                par = b.n % 2
                for k in range(TOPK):
                    pool.indirect_dma_start(y_got[:, j % NYG, k, :], None, y_slots[par], at_slots(y_slots, par, j, k)
                                            ).then_inc(s_got[j % NYG], 16)

            def body(b):
                if b.prep:
                    scatter(b)
                elif b.units:
                    pass_fence(b.g * FENCES + 1)
                if b.units:
                    for i in range(NYS):
                        pool.wait_ge(s_yw[i], (b.g + 1) * (16 * NPAIR // NYS))
                    if b.n > 0:
                        pool.wait_ge(s_r, b.g * NJ)
                    pass_fence(b.g * FENCES + 2)
                    for j in range(NYG):
                        gather(b, j)
                    if b.prep:
                        scatter_tiles((b.n + 1) % 2, range(SCAT_FIRST, NJ))
                    for j in range(NYG, NJ):
                        pool.wait_ge(s_r, b.g * NJ + j - NYG + 1)
                        pass_fence(b.g * FENCES + 3 + j - NYG)
                        gather(b, j)

            pool.wait_ge(s_zero[0], 16)
            pool.wait_ge(s_chain, SLOT_LINK)
            nc.gpsimd.tensor_tensor(fence_pool[:], zeros[:, 0:1], zeros[:, 1:2], ALU.mult).then_inc(s_fence, 1)
            scatter_tiles(0, range(NJ))
            pool.wait_ge(s_up, 3)
            clear_slots(1)
            run_bodies(pool, body)

        @block.scalar
        def _(act):
            act.dma_start(cond_in[:], cond).then_inc(s_cond, 16)
            act.dma_start(rw[:], router_w.rearrange("(k p) e -> p k e", p=P)).then_inc(s_rw, 16)
            nc.scalar.preload_act_table(ACT.Sigmoid)
            act.dma_start(rbias[:], router_b.rearrange("(a e) -> a e", a=1).broadcast_to([P, E])
                          ).then_inc(s_rbias, 16)

            def act_turn_x(b, i):
                g, par = b.g + 1, (b.n + 1) % 2
                half, kc = i // KC, i % KC
                act.wait_ge(s_turnx, g * 4 + i + 1)
                if b.n >= 1:
                    act.wait_ge(s_z, (b.g * 2 - 1 + half) * KC)
                    act.wait_ge(s_up, b.g * NU)
                cols = slice(half * G, (half + 1) * G)
                src = turn_bank(b, i)
                nc.scalar.activation(xq[:, par, kc, cols], src[:], ACT.Copy, scale=0.5)
                nc.scalar.activation(xs[0][:, par, kc, cols], src[:], ACT.Copy, scale=0.5).then_inc(s_xhi, 1)

            def act_sigmoid(b):
                act.wait_ge(s_lg, b.g + 2)
                if b.n >= 0:
                    act.wait_ge(s_comb, b.g + 1)
                nc.scalar.activation(sg[:], lg[:], ACT.Sigmoid).then_inc(s_sg, 1)
                nc.scalar.preload_act_table(ACT.Gelu)

            def act_out(b, part):
                g = b.g - (2 if part == 3 else 1)
                n = b.n - (2 if part == 3 else 1)
                act.wait_ge(s_turno, g * 4 + part + 1)
                if part >= 2:
                    act.wait_ge(s_out[part - 2], (g + 1) * (16 * TT))
                elif n >= 1:
                    act.wait_ge(s_out[part + 2], g * (16 * TT))
                nc.scalar.activation(o_tok[:, part % 2].rearrange("p j c -> p (j c)"),
                                     spare[:], ACT.Copy).then_inc(s_otok, 1)

            def pair_high(b, p, ahead=0):
                g, n = b.g + ahead, b.n + ahead
                act.wait_ge(s_xt, g * NPAIR + p + 1)
                if p >= 2:
                    act.wait_ge(s_up, g * NU + p - 1)
                elif n > 0:
                    act.wait_ge(s_up, g * NU - NU + NPAIR - 2 + p + 1)
                nc.scalar.activation(xe[0][:, p % 2].rearrange("p k s -> p (k s)"), pair_bank(p)[:], ACT.Copy, scale=0.5
                                     ).then_inc(s_xehi, 1)

            def hid_free(b, u):
                if b.n > 0 or u >= NR:
                    act.wait_ge(s_down, b.g * NU + u - NR + 1)

            def gelu(b, u):
                act.wait_ge(s_up, b.g * NU + u + 1)
                if u >= 2:
                    act.wait_ge(s_lo, b.g * NU + u - 1)
                elif b.n > 0:
                    act.wait_ge(s_lo, b.g * NU - NU + NPAIR - 2 + u + 1)
                src = ring_bank("up", u)
                nc.scalar.activation(act32[:, u % 2], src[:], ACT.Gelu, scale=1.0 / UP)
                hid_free(b, u)
                nc.scalar.activation(hid[0][:, u % NR], src[:], ACT.Gelu, scale=1.0 / UP).then_inc(s_hi, 1)

            def result(b, p):
                act.wait_ge(s_down, b.g * NU + p + 1)
                if p >= NYS or b.n > 0:
                    act.wait_ge(s_yw[p % NYS], b.g * (16 * NPAIR // NYS) + p // NYS * 16)
                nc.scalar.activation(y_pair[:, p % NYS], ring_bank("down", p)[:], ACT.Copy).then_inc(s_ev, 1)

            def tanh(b, u):
                act.wait_ge(s_up, b.g * NU + u + 1)
                n = n_sha[u] - 1
                if b.n > 0 or n >= 1:
                    act.wait_ge(s_su, b.g * NSH + n)
                nc.scalar.activation(half32[:], ring_bank("first", u)[:], ACT.Tanh, scale=0.5 / UP
                                     ).then_inc(s_tanh, 1)

            def shared_high(b, back, u):
                g = b.g - back
                act.wait_ge(s_prod, g * NSH + n_sha[u])
                act.wait_ge(s_down, g * NU + u - NR + 1)
                nc.scalar.activation(hid[0][:, u % NR], prod32[:, n_sha[u] % 2], ACT.Copy).then_inc(s_hi, 1)

            def act_z(b, back, half):
                g = b.g - back
                act.wait_ge(s_z, (g * 2 + half + 1) * KC)
                nc.scalar.activation(flat(zs[0][:, half]), flat(zq[:, (b.n - back) % 2, half * TG:(half + 1) * TG]),
                                     ACT.Copy).then_inc(s_zhi, 1)

            def act_gate(b, s):
                r = b.g - 1
                act.wait_ge(s_step, r * TS + s + 1)
                nc.scalar.activation(flat3(th[:, s % 2, :, :, 1]), gate_sums(s), ACT.Tanh, scale=0.5 / UP
                                     ).then_inc(s_th, 1)

            def act_h(b, s):
                r = b.g - 1
                act.wait_ge(s_pre, r * TS + s + 1)
                if b.n > 1 and s % HALF == 0:
                    act.wait_ge(s_och, r * 4 - 4 + s // HALF + 1)
                src = flat3(pre[:, s % 2, :, :, 1])
                nc.scalar.activation(flat3(hs[0][:, s % 2]), src, ACT.Tanh).then_inc(s_hhi, 1)
                nc.scalar.activation(flat3(hist[:, s]), src, ACT.Tanh).then_inc(s_h, 1)

            def misc(b, u):
                if u in MISC and b.there(*MISC[u], b.n):
                    what, part = MISC[u]
                    if what == TURN_X:
                        act_turn_x(b, part)
                    elif what == OUT:
                        act_out(b, part)

            def body(b):
                for u, (kind, _) in enumerate(UNITS):
                    if u == 0 and b.tail:
                        shared_high(b, 1, NU - 1)
                    if b.units and u + 1 < NPAIR:
                        pair_high(b, u + 1)
                    if b.units and kind == EXPERT:
                        gelu(b, u)
                    for half in (0, 1):
                        s = STEP_AT.get((u, half)) if b.tail else None
                        if s is not None:
                            act_gate(b, s)
                        if half == 0 and b.units and u > NPAIR:
                            shared_high(b, 0, u - 1)
                        if s is not None:
                            act_h(b, s)
                        if half == 0:
                            if b.units and kind == SHARED:
                                tanh(b, u)
                            misc(b, u)
                            if b.units and 0 <= u - DOWN_LAG < NPAIR:
                                result(b, u - DOWN_LAG)
                    if u == 3 and b.tail:
                        act_z(b, 1, 1)
                    if u == 18 and b.units:
                        act_z(b, 0, 0)
                    if u == 7 and b.prep:
                        act_sigmoid(b)
                    for n in range(len(CONV)):
                        if b.n == 0 and CONV_SLOT[n] == u:
                            conv(n)
                    if b.n == 0 and u == 16:
                        recurrence_setup()
                if b.prep:
                    pair_high(b, 0, 1)

            def conv(n):
                _, dst, a, k, w = conv_parts(CONV[n])
                act.wait_ge(s_stage[n % NSTAGE], 16 * (n // NSTAGE + 1))
                nc.scalar.activation(dst[0], stage[:, n % NSTAGE, 0:a * k * w], ACT.Copy, scale=WUP
                                     ).then_inc(s_convhi, 1)

            def recurrence_setup():
                for i in range(2):
                    act.wait_ge(s_turn0, i + 1)
                    nc.scalar.activation(flat3(gwt[0][:, KC * i:KC * i + KC]), gate_ps[i][:], ACT.Copy,
                                         scale=(UP, WUP)[i]).then_inc(s_gwhi, 1)
                nc.scalar.activation(hs[0][:, 1], cond_t[:, :, 0, :], ACT.Copy).then_inc(s_hhi, 1)
                nc.scalar.activation(hist[:, TS - 1], cond_t[:, :, 0, :], ACT.Copy).then_inc(s_h, 1)

            act.wait_ge(s_condt, 1)
            prologue = Body(-1, -1)
            for i in range(4):
                act_turn_x(prologue, i)
            act_sigmoid(prologue)
            for n in range(N_EXPERT_CONV):
                conv(n)
            pair_high(prologue, 0, 1)
            run_bodies(act, body)

        @block.vector
        def _(dve):
            done = [0]

            def link(ins):
                done[0] += 1
                ins.then_inc(s_const, 1)
                dve.wait_ge(s_const, done[0])

            def low_x(b, i):
                g, par = b.g + 1, (b.n + 1) % 2
                half, kc = i // KC, i % KC
                cols = slice(half * G, (half + 1) * G)
                dve.wait_ge(s_xhi, g * 4 + i + 1)
                dve.tensor_tensor(xs[1][:, par, kc, cols], xq[:, par, kc, cols], xs[0][:, par, kc, cols],
                                  ALU.subtract).then_inc(s_xlo, 1)

            def logits(b):
                g = b.g + 1
                dve.wait_ge(s_lgps, g + 1)
                if b.n >= 0:
                    dve.wait_ge(s_sg, g)
                dve.scalar_tensor_tensor(lg[:], spare[:, 0:NJ * E].rearrange("p (j e) -> p j e", e=E), 1.0 / UP,
                                         every_tile(cond_lg), ALU.mult, ALU.add).then_inc(s_lg, 1)

            def chain(s, g, steps, first, last):
                for n in range(first, last + 1):
                    if n > 0:
                        dve.wait_ge(s, g * (len(steps) - 1) + n)
                    for i in steps[n]:
                        ins = i()
                    if n < len(steps) - 1:
                        ins.then_inc(s, 1)
                return ins

            each = range(NJ)
            tt, ts = dve.tensor_tensor, dve.tensor_scalar
            ROUTE = [
                [lambda: tt(sel[:, :, 0:E], sg[:], every_tile(rbias), ALU.add)],
                [lambda: dve.memset(fence[:], 0.0)] + [lambda j=j: dve.max(top8[:, j], sel[:, j, 0:E]) for j in each],
                [lambda: dve.tensor_copy(seek[:, :, 0:TOPK], top8[:, :, 0:TOPK])],
                [lambda: dve.memset(fence[:], 0.0)] + [lambda j=j: dve.match_replace(left[:, j], seek[:, j], sel[:, j],
                                                                                     TAKEN) for j in each],
                [lambda: tt(mask16[:], left[:, :, 0:E], sel[:, :, 0:E], ALU.not_equal),
                 lambda: tt(mask[:], left[:, :, 0:E], sel[:, :, 0:E], ALU.not_equal)],
                [lambda: tt(smask[:], mask[:], sg[:], ALU.mult)],
                [lambda: dve.tensor_reduce(den[:], smask[:], AX_X, ALU.add)],
                [lambda: ts(deps[:], den[:], 1e-9, None, ALU.add),
                 lambda: ts(okay[:], den[:], 1e-9, None, ALU.is_gt)],
                [lambda: dve.reciprocal(drec[:], deps[:]),
                 lambda: ts(alt[:], okay[:], -1.0 / TOPK, 1.0 / TOPK, ALU.mult, ALU.add)],
                [lambda: tt(part_b[:], mask[:], bcast(alt), ALU.mult),
                 lambda: tt(okrec[:], drec[:], okay[:], ALU.mult)],
                [lambda: tt(part_a[:], smask[:], bcast(okrec), ALU.mult)],
                [lambda: tt(comb[:], part_a[:], part_b[:], ALU.add)],
            ]

            def route(b, first, last):
                g = b.g + 1
                if first == 0:
                    dve.wait_ge(s_sg, g + 1)
                    if b.n >= 0:
                        dve.wait_ge(s_rkps, g)
                assert len(ROUTE) == N_ROUTE_LINKS + 1
                ins = chain(s_route, g, ROUTE, first, last)
                if last == len(ROUTE) - 1:
                    ins.then_inc(s_comb, 1)

            def place_steps(par):
                counts = ranks[:, NJ * E:].rearrange("p (e a) -> p e a", a=1).broadcast_to([P, E, 8])
                rank = ranks[:, 0:NJ * E].rearrange("p (j e) -> p j e", e=E)
                owner_pair = owner_c[:].rearrange("p (n i) -> p n i", i=2)
                over = lambda ap: ap.rearrange("p (a e) -> p a e", a=1).broadcast_to([P, NT, E])
                return [
                    [lambda: tt(opened[:], counts, full_at[:].rearrange("p (a k) -> p a k", a=1).broadcast_to([P, E, 8]),
                                ALU.is_gt)],
                    [lambda: dve.tensor_reduce(scan[0][:, E:], opened[:], AX_X, ALU.add)],
                    [lambda: tt(scan[1][:, E:], scan[0][:, E:], scan[0][:, E - 1:2 * E - 1], ALU.add)],
                    [lambda: tt(scan[2][:, E:], scan[1][:, E:], scan[1][:, E - 2:2 * E - 2], ALU.add)],
                    [lambda: tt(tile_end[:], scan[2][:, E:], scan[2][:, E - 4:2 * E - 4], ALU.add)],
                    [lambda: tt(past[:], tile_no[:].rearrange("p (i a) -> p i a", a=1).broadcast_to([P, NT, E]),
                                over(tile_end[:]), ALU.is_ge),
                     lambda: tt(tile_base[:], tile_end[:], scan[0][:, E:], ALU.subtract)],
                    [lambda: dve.tensor_reduce(owner_f[:], past[:], AX_X, ALU.add),
                     lambda: dve.scalar_tensor_tensor(slot[:], every_tile(tile_base), float(P), rank, ALU.mult, ALU.add)],
                    [lambda: ts(owner_c[:], owner_f[:], float(E - 1), None, ALU.min),
                     lambda: dve.scalar_tensor_tensor(slot_up[:], slot[:], 1.0, mask[:], ALU.add, ALU.mult),
                     lambda: dve.scalar_tensor_tensor(slot_dn[:], slot[:], FAR, mask[:], ALU.subtract, ALU.mult)],
                    [lambda: dve.scalar_tensor_tensor(owner[:, par], owner_pair[:, :, 1], float(E), owner_pair[:, :, 0],
                                                      ALU.mult, ALU.add),
                     lambda: dve.tensor_reduce(top_slot[:], slot_up[:], AX_X, ALU.max),
                     lambda: dve.tensor_reduce(low_slot[:], slot_dn[:], AX_X, ALU.min)],
                    [lambda: ts(where[:, par, :, 1], top_slot[:], 1.0, None, ALU.subtract),
                     lambda: ts(where[:, par, :, 0], low_slot[:], FAR, None, ALU.add),
                     lambda: tt(is_top[:], slot_up[:], bcast(top_slot), ALU.is_equal),
                     lambda: tt(is_low[:], slot_dn[:], bcast(low_slot), ALU.is_equal)],
                    [lambda: tt(gate_top[:], is_top[:], comb[:], ALU.mult),
                     lambda: tt(gate_low[:], is_low[:], comb[:], ALU.mult)],
                    [lambda: dve.tensor_reduce(gate2[:, par, :, 1], gate_top[:], AX_X, ALU.add),
                     lambda: dve.tensor_reduce(gate2[:, par, :, 0], gate_low[:], AX_X, ALU.add)],
                ]

            N_PLACE = N_PLACE_LINKS + 1

            def place(b, first, last):
                g = b.g + 1
                if first == 0:
                    dve.wait_ge(s_rkps, g + 1)
                    dve.tensor_copy(ranks[:], spare[:, 0:NJ * E + E]).then_inc(s_rk, 1)
                    dve.wait_ge(s_rk, g + 1)
                    dve.wait_ge(s_comb, g + 1)
                ins = chain(s_chain, g, place_steps((b.n + 1) % 2), first, last)
                if last == N_PLACE - 1:
                    ins.then_inc(s_placed, 1)

            def pair_low(b, p, ahead=0):
                g = b.g + ahead
                dve.wait_ge(s_xehi, g * NPAIR + p + 1)
                dve.scalar_tensor_tensor(xe[1][:, p % 2].rearrange("p k s -> p (k s)"), pair_bank(p)[:], 0.5,
                                         xe[0][:, p % 2].rearrange("p k s -> p (k s)"), ALU.mult, ALU.subtract
                                         ).then_inc(s_xelo, 1)

            def product(b, u):
                n = n_sha[u] - 1
                if n >= 2:
                    dve.wait_ge(s_lo, b.g * NU + u - 1)
                elif b.n > 0:
                    dve.wait_ge(s_lo, b.g * NU - 2 + n + 1)
                dve.wait_ge(s_tanh, b.g * NSH + n + 1)
                buf = prod32[:, (n + 1) % 2]
                dve.scalar_tensor_tensor(buf, half32[:], 1.0, ring_bank("first", u)[:], ALU.add, ALU.mult
                                         ).then_inc(s_su, 1)
                dve.wait_ge(s_su, b.g * NSH + n + 1)
                dve.scalar_tensor_tensor(buf, buf, 0.5 / (UP * UP), ring_bank("second", u)[:], ALU.mult, ALU.mult
                                         ).then_inc(s_prod, 1)

            def low(b, back, u):
                g = b.g - back
                dve.wait_ge(s_hi, g * NU + u + 1)
                if b.n - back > 0 or u >= NR:
                    dve.wait_ge(s_down, g * NU + u - NR + 1)
                full = act32[:, u % 2] if u < NPAIR else prod32[:, n_sha[u] % 2]
                dve.tensor_tensor(hid[1][:, u % NR], full, hid[0][:, u % NR], ALU.subtract).then_inc(s_lo, 1)

            GATED_AT = {(0, 15, 0): (0, 0), (0, 15, 1): (0, 1), (0, 16, 0): (0, 2), (0, 16, 1): (0, 3),
                        (1, 0, 0): (1, 1), (1, 0, 1): (1, 2), (1, 1, 0): (1, 3)}

            def gated(b, back, half, i):
                g = b.g - back
                n = b.n - back
                j = half * NYG + i
                if i == 0 and half == 0:
                    dve.wait_ge(s_placed, g + 1)
                if i == 0 and (n > 0 or half > 0):
                    dve.wait_ge(s_y, g * 2 + half)
                dve.wait_ge(s_got[i], (g * 2 + half + 1) * (16 * TOPK))
                dve.tensor_scalar(r_part[:, i % 2], y_got[:, i, 0], gate2[:, n % 2, j, 0:1], None, ALU.mult
                                  ).then_inc(s_rp, 1)
                dve.wait_ge(s_rp, g * NJ + j + 1)
                dve.scalar_tensor_tensor(r_sum[:, i], y_got[:, i, 1], gate2[:, n % 2, j, 1:2], r_part[:, i % 2],
                                         ALU.mult, ALU.add).then_inc(s_r, 1)

            def residual(b, back, half):
                g, par = b.g - back, (b.n - back) % 2
                dve.wait_ge(s_y, g * 2 + half + 1)
                for kc in range(KC):
                    dve.scalar_tensor_tensor(zq[:, par, half * TG:(half + 1) * TG, kc, :],
                                             y_ps[kc][:].rearrange("p (t b) -> p t b", b=NB), MEAN,
                                             xq[:, par, kc, half * G:(half + 1) * G].rearrange("p (t b) -> p t b", b=NB),
                                             ALU.mult, ALU.add).then_inc(s_z, 1)

            def low_z(b, back, half):
                g, par = b.g - back, (b.n - back) % 2
                dve.wait_ge(s_zhi, g * 2 + half + 1)
                dve.tensor_tensor(flat(zs[1][:, half]), flat(zq[:, par, half * TG:(half + 1) * TG]),
                                  flat(zs[0][:, half]), ALU.subtract).then_inc(s_zlo, 1)

            def rec_rest(b, s):
                dve.tensor_copy(flat3(zr[:, s % 2, :, :, 0]), flat3(zq[:, (b.n - 1) % 2, s]))
                for kc in range(KC):
                    last = dve.scalar_tensor_tensor(zr[:, s % 2, kc, :, 1], hist[:, (s - 1) % TS, kc], leak[:, kc:kc + 1],
                                                    zq[:, (b.n - 1) % 2, s, kc], ALU.mult, ALU.add)
                last.then_inc(s_rest, 1)

            def rec_pre(b, s):
                r = b.g - 1
                if s == 0:
                    rec_rest(b, 0)
                dve.wait_ge(s_rest, r * TS + s + 1)
                dve.wait_ge(s_th, r * TS + s + 1)
                every = lambda ap: ap.rearrange("p k b i -> p (k b i)")
                dve.tensor_tensor_scan(every(pre[:, s % 2]), every(th[:, s % 2]), every(zr[:, s % 2]), 0.0,
                                       ALU.mult, ALU.add).then_inc(s_pre, 1)

            def rec_low(b, s):
                r = b.g - 1
                dve.wait_ge(s_h, r * TS + s + 2)
                dve.tensor_tensor(flat3(hs[1][:, s % 2]), flat3(hist[:, s]), flat3(hs[0][:, s % 2]),
                                  ALU.subtract).then_inc(s_hlo, 1)
                if s + 1 < TS:
                    rec_rest(b, s + 1)

            def out_channels(b, part):
                back = 2 if part == 3 else 1
                g, par = b.g - back, (b.n - back) % 2
                if part > 0 or b.n > 1:
                    dve.wait_ge(s_turno, g * 4 + part)
                dve.wait_ge(s_h, g * TS + (part + 1) * HALF + 1)
                quarter = slice(part * HALF, (part + 1) * HALF)
                for kc in range(KC):
                    ins = dve.scalar_tensor_tensor(o_ch[:, kc], zq[:, par, quarter, kc, :], 2.0,
                                                   hist[:, quarter, kc, :], ALU.mult, ALU.add)
                ins.then_inc(s_och, 1)

            def body(b):
                for u, (kind, _) in enumerate(UNITS):
                    if u == 0 and b.tail:
                        low(b, 1, NU - 1)
                        gated(b, 1, 1, 0)
                    if b.units and u + 1 < NPAIR:
                        pair_low(b, u + 1)
                    if u == 18 and b.units:
                        residual(b, 0, 0)
                    for half in (0, 1):
                        s = STEP_AT.get((u, half)) if b.tail else None
                        if s is not None:
                            rec_pre(b, s)
                        if half == 0 and b.units:
                            if kind == EXPERT:
                                low(b, 0, u)
                            elif u > NPAIR:
                                low(b, 0, u - 1)
                        if s is not None:
                            rec_low(b, s)
                        if half == 0:
                            if b.units and kind == SHARED:
                                product(b, u)
                            if u in MISC and MISC[u][0] == TURN_X and b.prep:
                                low_x(b, MISC[u][1])
                        if b.tail and (u, half) == (2, 0):
                            residual(b, 1, 1)
                        if b.prep and (u, half) == (8, 0):
                            route(b, 6, len(ROUTE) - 1)
                        if b.prep and (u, half) == (10, 0):
                            place(b, 4, 7)
                        for back, there in ((1, b.tail), (0, b.units)):
                            if there and (back, u, half) in GATED_AT:
                                gated(b, back, *GATED_AT[back, u, half])
                    if b.tail:
                        if u == 4:
                            low_z(b, 1, 1)
                    if b.late and u == 5:
                        out_channels(b, 3)
                    for part, at in enumerate((7, 11, 17)):
                        if b.tail and u == at:
                            out_channels(b, part)
                    if b.prep:
                        if u == 6:
                            logits(b)
                        if u == 7:
                            route(b, 0, 5)
                        if u == 9:
                            place(b, 0, 3)
                        if u == 10:
                            place(b, 8, N_PLACE - 1)
                    if b.units:
                        if u == 18:
                            low_z(b, 0, 0)
                    for n in range(len(CONV)):
                        if b.n == 0 and CONV_SLOT[n] == u:
                            conv(n)
                    if b.n == 0 and u == 14:
                        constants()
                    if b.n == 0 and u == 16:
                        recurrence_setup()
                if b.prep:
                    pair_low(b, 0, 1)

            def conv(n):
                _, dst, a, k, w = conv_parts(CONV[n])
                dve.wait_ge(s_convhi, n + 1)
                dve.scalar_tensor_tensor(dst[1], stage[:, n % NSTAGE, 0:a * k * w], WUP, dst[0],
                                         ALU.mult, ALU.subtract).then_inc(s_conv, 1)

            def constants():
                dve.wait_ge(s_small, 16 * 3)
                link(dve.memset(ones2[:], 1.0))
                link(dve.memset(th[:], 0.0))
                link(dve.tensor_scalar(leak[:], al[:], -1.0, 1.0, ALU.mult, ALU.add))
                link(dve.tensor_scalar(gb_full[:], gb_in[:], UP, None, ALU.mult))
                link(dve.tensor_copy(gb_hi[:], gb_full[:]))
                link(dve.tensor_tensor(gb_lo[:], gb_full[:], gb_hi[:], ALU.subtract))
                link(dve.tensor_scalar(gb_lo2[:], gb_lo[:], ident[0:2, 1:2], None, ALU.mult))
                link(dve.scalar_tensor_tensor(gb[:], gb_hi[:], ident[0:2, 0:1], gb_lo2[:], ALU.mult, ALU.add))
                assert done[0] == N_CONST

            def recurrence_setup():
                for i in range(2):
                    dve.wait_ge(s_gwhi, i + 1)
                    dve.scalar_tensor_tensor(flat3(gwt[1][:, KC * i:KC * i + KC]), gate_ps[i][:], (UP, WUP)[i],
                                             flat3(gwt[0][:, KC * i:KC * i + KC]), ALU.mult, ALU.subtract
                                             ).then_inc(s_gwlo, 1)
                dve.wait_ge(s_h, 1)
                dve.tensor_tensor(flat3(hs[1][:, 1]), flat3(hist[:, TS - 1]), flat3(hs[0][:, 1]),
                                  ALU.subtract).then_inc(s_hlo, 1)

            link(dve.memset(sel[:], PAD))
            link(dve.memset(seek[:], PAD))
            for part in scan:
                link(dve.memset(part[:, 0:E], 0.0))
            link(dve.memset(ones16[:], 1.0))
            dve.wait_ge(s_clg_ps, 1)
            for t in range(TT):
                ins = dve.tensor_copy(cond_t[:, :, t, :], bank[0][:, 0:STEP].rearrange("p (k b) -> p k b", k=KC))
            ins.then_inc(s_condt, 1)
            dve.wait_ge(s_rw, 16)
            link(dve.tensor_scalar(rwx[0][:], rw[:, 0:KC, :], WUP, None, ALU.mult))
            link(dve.scalar_tensor_tensor(rwx[1][:], rw[:, 0:KC, :], WUP, rwx[0][:], ALU.mult, ALU.subtract))
            assert done[0] == N_ROUTER_CONST
            prologue = Body(-1, -1)
            for i in range(4):
                low_x(prologue, i)
            dve.wait_ge(s_clg_ps, 2)
            link(dve.tensor_copy(cond_lg[:], bank[1][:, 0:E]))
            logits(prologue)
            dve.wait_ge(s_rbias, 16)
            route(prologue, 0, len(ROUTE) - 1)
            dve.wait_ge(s_ident, 6)
            place(prologue, 0, N_PLACE - 1)
            for n in range(N_EXPERT_CONV):
                conv(n)
            pair_low(prologue, 0, 1)
            run_bodies(dve, body)

        @block.tensor
        def _(pe):
            def mm(out_ap, w, mov, start, stop):
                return pe.matmul(out_ap, w, mov, start=start, stop=stop, skip_group_check=True)

            def pairs(out_ap, w, mov, start, stop, chunks, beside=None):
                last, n = None, len(chunks) * 3
                for i, k in enumerate(chunks):
                    if beside and i == len(chunks) - 1:
                        beside()
                    for j, (a, c) in enumerate(((0, 0), (1, 0), (0, 1))):
                        last = mm(out_ap, w(a, k), mov(c, k), start and i == 0 and j == 0, stop and i * 3 + j == n - 1)
                return last

            experts = {}

            def load_experts(b, p):
                both = pe.value_load(owner[0:1, b.n % 2, p:p + 1], min_val=0, max_val=E * E - 1)
                experts[p % 4, 0], experts[p % 4, 1] = both % E, both // E

            def up_expert(b, u):
                if b.n == 0 and u == 0:
                    pe.wait_ge(s_conv, N_EXPERT_CONV)
                pe.wait_ge(s_xelo, b.g * NPAIR + u + 1)
                ring_free(pe, b, "up", u)
                dst = ring_bank("up", u)
                for i in range(2):
                    v = experts[u % 4, i]
                    for h in range(2):
                        last = pairs(dst[:, (h * 2 + i) * P:(h * 2 + i + 1) * P],
                                     lambda a, k: w1e_s[a][:, v, k, h * P:(h + 1) * P],
                                     lambda c, k: xe[c][:, u % 2, k, i * P:(i + 1) * P],
                                     True, True, range(KC))
                last.then_inc(s_up, 1)

            def down_expert(b, u):
                pe.wait_ge(s_lo, b.g * NU + u + 1)
                ring_free(pe, b, "down", u)
                dst = ring_bank("down", u)
                for i in range(2):
                    v = experts[u % 4, i]
                    last = pairs(dst[:, i * C:(i + 1) * C],
                                 lambda a, h: hid[a][:, u % NR, (h * 2 + i) * P:(h * 2 + i + 1) * P],
                                 lambda c, h: w2e_s[c][:, v, h, :], True, True, range(KC))
                last.then_inc(s_down, 1)

            def up_shared(b, u, beside):
                half, m = divmod(UNITS[u][1], MID)
                if u == NPAIR:
                    pe.wait_ge(s_xlo, b.g * 4 + 4)
                    if b.n == 0:
                        pe.wait_ge(s_conv, len(CONV))
                for i, what in enumerate(("first", "second")):
                    ring_free(pe, b, what, u)
                    last = pairs(ring_bank(what, u)[:], lambda a, k: w13_s[a][:, i, k, m * P:(m + 1) * P],
                                 lambda c, k: xs[c][:, b.n % 2, k, half * G:(half + 1) * G], True, True, range(KC),
                                 beside if i == 1 else None)
                last.then_inc(s_up, 1)

            def down_shared(b, back, u):
                half, m = divmod(UNITS[u][1], MID)
                g = b.g - back
                pe.wait_ge(s_lo, g * NU + u + 1)
                if m == 0 and half == 0:
                    pe.wait_ge(s_xelo, g * NPAIR + NPAIR)
                elif m == 0:
                    pe.wait_ge(s_z, (g * 2 + half) * KC)
                for kc in range(KC):
                    last = pairs(y_ps[kc][:], lambda a, k: w2_s[a][:, m, kc * P:(kc + 1) * P],
                                 lambda c, k: hid[c][:, u % NR], m == 0, False, [0])
                last.then_inc(s_down, 1)

            def add_routed(b, back, half):
                g = b.g - back
                for j in range(NYG):
                    pe.wait_ge(s_r, g * NJ + half * NYG + j + 1)
                    for kc in range(KC):
                        last = mm(y_ps[kc][:, j * P:(j + 1) * P], r_sum[:, j, kc * P:(kc + 1) * P], ident[:],
                                  False, j == NYG - 1)
                last.then_inc(s_y, 1)

            def gate_fill(b, back, half, hf):
                g = b.g - back
                n = b.n - back
                if n == 0 and half == 0 and hf == 0:
                    pe.wait_ge(s_gwlo, 2)
                    pe.wait_ge(s_const, N_CONST)
                pe.wait_ge(s_zlo, g * 2 + half + 1)
                if n > 0 or half > 0:
                    pe.wait_ge(s_th, (g * 2 + half) * TG - (0 if hf else HALF))
                for jc in range(KC):
                    cols = slice(jc * P, (jc + 1) * P)
                    dst = gate_ps[hf][:].rearrange("p (t k b) -> p t k b", k=KC, b=NB)[:, :, jc, :]
                    mm(dst, gb[:, cols], ones2[:].rearrange("p (t b) -> p t b", b=NB), jc == 0, False)
                    pairs(dst, lambda a, k: gwt[a][:, KC + k, cols],
                          lambda c, k: zs[c][:, half, hf * HALF:(hf + 1) * HALF, k, :], False, False, range(KC))

            def gate_step(b, s):
                r = b.g - 1
                for c, weights, ready in ((0, (0, 1), s_hhi), (1, (0,), s_hlo)):
                    pe.wait_ge(ready, r * TS + s + 1)
                    for jc in range(KC):
                        for a in weights:
                            for k in range(KC):
                                last = mm(gate_sums(s)[:, jc * NB:(jc + 1) * NB], gwt[a][:, k, jc * P:(jc + 1) * P],
                                          hs[c][:, (s - 1) % 2, k, :], False, False)
                last.then_inc(s_step, 1)

            def turn_pair(b, p, ahead=0):
                g = b.g + ahead
                if ahead or p < OWN_TURN:
                    released(pe, b, SPARE.index((FIRST, 0, NU - 1) if ahead else (TOKENS, p, p - 1)))
                elif p >= OWN_TURN + 2:
                    pe.wait_ge(s_xelo, g * NPAIR + p - 1)
                elif b.n > 0:
                    pe.wait_ge(s_z, g * 2 * KC)
                pe.wait_ge(s_xin[p % NIN], g * (16 * NPAIR // NIN) + (p // NIN + 1) * 16)
                for k in range(KC):
                    for i in range(2):
                        last = pe.transpose(pair_bank(p)[:, (k * 2 + i) * P:(k * 2 + i + 1) * P],
                                            x_pair[:, p % NIN, i, k * P:(k + 1) * P], ident[:])
                last.then_inc(s_xt, 1)

            def misc(b, u):
                if u not in MISC or not b.there(*MISC[u], b.n):
                    return
                what, part = MISC[u]
                if b.n >= 0 or what != TURN_X:
                    released(pe, b, SPARE.index((what, part, u)))
                g, par = b.g + 1, (b.n + 1) % 2
                if what == TURN_X:
                    half, k = divmod(part, KC)
                    if part == 0:
                        pe.wait_ge(s_x[par], loads(b) * (16 * TT))
                    for j in range(NJ // 2):
                        last = pe.transpose(turn_bank(b, part)[:, j * P:(j + 1) * P],
                                            x_tok[:, par, half * (NJ // 2) + j, k * P:(k + 1) * P], ident[:])
                    last.then_inc(s_turnx, 1)
                elif what == LOGITS:
                    pe.wait_ge(s_xlo, g * 4 + 4)
                    for j in range(NJ):
                        last = pairs(spare[:, j * E:(j + 1) * E],
                                     lambda a, k: xs[a][:, par, k, j * P:(j + 1) * P],
                                     lambda c, k: rwx[c][:, k, :], True, True, range(KC))
                    last.then_inc(s_lgps, 1)
                elif what == RANKS:
                    pe.wait_ge(s_route, (b.g + 1) * N_ROUTE_LINKS + MASK_LINK)
                    chosen = mask16[:].rearrange("p j e -> p (j e)")
                    mm(spare[:, 0:NJ * E], below[:], chosen, True, False)
                    for d in range(1, NJ):
                        mm(spare[:, d * E:NJ * E], ones16[:], chosen[:, 0:(NJ - d) * E], False, False)
                    for j in range(NJ):
                        last = mm(spare[:, NJ * E:NJ * E + E], ones16[:], mask16[:, j, :], False, j == NJ - 1)
                    last.then_inc(s_rkps, 1)
                else:
                    g = b.g - (2 if part == 3 else 1)
                    pe.wait_ge(s_och, g * 4 + part + 1)
                    for j in range(2):
                        for kc in range(KC):
                            last = pe.transpose(spare[:, j * C + kc * P:j * C + (kc + 1) * P],
                                                o_ch[:, kc, j * TT:(j + 1) * TT, :].rearrange("p t b -> p (t b)"),
                                                ident[:])
                    last.then_inc(s_turno, 1)

            def body(b):
                for u, (kind, _) in enumerate(UNITS):
                    step = (lambda: gate_step(b, STEP_AT[(u, 0)])) if b.tail and (u, 0) in STEP_AT else None
                    if u == 0 and b.tail:
                        down_shared(b, 1, NU - DOWN_LAG)
                    if u == 0 and b.units:
                        load_experts(b, 0)
                    if b.units and u + 1 < NPAIR:
                        turn_pair(b, u + 1)
                    if b.units:
                        if kind == EXPERT:
                            up_expert(b, u)
                        else:
                            up_shared(b, u, step)
                    if step and (kind == EXPERT or not b.units):
                        step()
                    misc(b, u)
                    if u == 1 and b.tail:
                        down_shared(b, 1, NU - 1)
                    if b.units and u >= DOWN_LAG:
                        if u - DOWN_LAG < NPAIR:
                            down_expert(b, u - DOWN_LAG)
                        else:
                            down_shared(b, 0, u - DOWN_LAG)
                    if b.units and u + 1 < NPAIR:
                        load_experts(b, u + 1)
                    if b.tail and (u, 1) in STEP_AT:
                        gate_step(b, STEP_AT[(u, 1)])
                    if b.tail:
                        if u == 1:
                            add_routed(b, 1, 1)
                        for at, half, hf in ((2, 0, 1), (8, 1, 0), (12, 1, 1)):
                            if u == at:
                                gate_fill(b, 1, half, hf)
                    if b.units and u == 17:
                        add_routed(b, 0, 0)
                    if b.n == 0 and u == 15:
                        recurrence_setup()
                if b.units:
                    gate_fill(b, 0, 0, 0)
                if b.prep:
                    turn_pair(b, 0, 1)

            def recurrence_setup():
                pe.wait_ge(s_gw, 16)
                for i in range(2):
                    for k in range(KC):
                        for jc in range(KC):
                            c0 = (i * KC + k) * P
                            last = pe.transpose(gate_ps[i][:, k * C + jc * P:k * C + (jc + 1) * P],
                                                gw[:, jc, c0:c0 + P], ident[:])
                    last.then_inc(s_turn0, 1)

            pe.wait_ge(s_ident, 4)
            pe.wait_ge(s_cond, 16)
            for k in range(KC):
                last = pe.transpose(bank[0][:, k * NB:(k + 1) * NB], cond_in[:, k * P:(k + 1) * P],
                                    ident[0:NB, 0:NB])
            last.then_inc(s_clg_ps, 1)
            prologue = Body(-1, -1)
            for u in (2, 3, 4, 5):
                misc(prologue, u)
            pe.wait_ge(s_condt, 1)
            pe.wait_ge(s_rw, 16)
            for k in range(KC):
                last = mm(bank[1][:, 0:E], cond_t[:, k].rearrange("p t b -> p (t b)"), rw[:, KC + k, :],
                          k == 0, k == KC - 1)
            last.then_inc(s_clg_ps, 1)
            pe.wait_ge(s_const, N_ROUTER_CONST)
            misc(prologue, 6)
            misc(prologue, 9)
            turn_pair(prologue, 0, 1)
            run_bodies(pe, body)


_INS = ['x', 'cond_1024', 'L0_cond_router_W', 'L0_cond_router_bias', 'L0_cond_w1', 'L0_cond_w3', 'L0_cond_w2',
        'L0_cond_W1e', 'L0_cond_W2e', 'L1_cond_W', 'L1_cond_b', 'L1_cond_alpha']
_OUTS = [((32, 256, 256), 'float32')]


def kernel(**inputs):
    import numpy as _np
    import concourse.bacc as _bacc
    from concourse import mybir as _mybir
    from concourse.bass_utils import run_bass_kernel_spmd as _run

    nc = _bacc.Bacc("TRN2", target_bir_lowering=False, num_devices=1)
    arrays, args = {}, []
    for name in _INS:
        a = _np.ascontiguousarray(inputs[name])
        arrays[f"in_{name}_dram"] = a
        args.append(nc.dram_tensor(f"in_{name}_dram", a.shape, _mybir.dt.from_np(a.dtype), kind="ExternalInput").ap())
    for i, (shape, dtype) in enumerate(_OUTS):
        dt = _mybir.dt.from_np(_np.dtype(dtype))
        args.append(nc.dram_tensor(f"out_{i}_dram", shape, dt, kind="ExternalOutput").ap())
    moe_gated_recurrence(nc, *args)
    r = _run(nc, [arrays], core_ids=[0])
    got = tuple(r.results[0][f"out_{i}_dram"] for i in range(len(_OUTS)))
    return got[0]
```
